# Optimizing a Trainium2 kernel written in Bass

```python
import numpy as np
import jax
import jax.numpy as jnp

def _softmax(x, axis=-1):
    return jax.nn.softmax(x, axis=axis)

def _gelu(x):
    return jax.nn.gelu(x, approximate=True)

def _silu(x):
    return jax.nn.silu(x)

def _sigmoid(x):
    return jax.nn.sigmoid(x)

def _layernorm(x, axis=-1, eps=1e-05):
    m = jnp.mean(x, axis=axis, keepdims=True)
    v = jnp.var(x, axis=axis, keepdims=True)
    return (x - m) / jnp.sqrt(v + eps)

def _scatter_add(tgt, idx, src, axis=0):
    return tgt.at[idx].add(src)

def _segment_sum(src, seg, n):
    return jax.ops.segment_sum(src, seg, n)
kernel_name = 'mk_xattn_ffn_d1_seqx_r2_b52df1'

def setup_inputs(seed: int=0):
    np.random.seed(seed)
    _w = jnp.asarray

    def _rec_inputs():
        import jax
        import jax.numpy as jnp
        _rk = jax.random.key(seed)
        x = -0.0003929 + 0.9999 * jax.random.normal(jax.random.fold_in(_rk, 1), (2, 1024, 2048), jnp.float32)
        _lenS = 1024 - jax.random.randint(jax.random.fold_in(_rk, 7), (2,), 0, max(1, 1024 // 4) + 1, jnp.int32)
        _lenS2 = 2048 - jax.random.randint(jax.random.fold_in(_rk, 8), (2,), 0, max(1, 2048 // 4) + 1, jnp.int32)
        pos_BxS = jnp.broadcast_to(jnp.arange(1024, dtype=jnp.int32), (2, 1024))
        _ctx_1024P = jax.random.normal(jax.random.fold_in(_rk, 12), (2, 16, 512), jnp.float32)
        _ctx_1024c = jax.random.dirichlet(jax.random.fold_in(_rk, 512), 0.3 * jnp.ones((16,), jnp.float32), (2, 2048))
        _ctx_1024t = jnp.einsum('bsk,bkd->bsd', _ctx_1024c, _ctx_1024P)
        _ctx_1024t = _ctx_1024t * jax.lax.rsqrt(jnp.mean(jnp.square(_ctx_1024t)) + 1e-12) * 0.953939
        ctx_1024 = 6.77073e-06 + 0.0199965 * (_ctx_1024t + 0.3 * jax.random.normal(jax.random.fold_in(_rk, 612), (2, 2048, 512), jnp.float32))
        return (x, pos_BxS, ctx_1024)
    x, pos_BxS, ctx_1024 = _rec_inputs()

    def _L0_xattn_setup():
        import jax, jax.numpy as jnp
        import numpy as np
        H = 512
        C = 4
        RH = 16
        HS = H // RH
        DR = 8
        M = 2048
        NH = 16
        HD = H // NH
        A_SIZE = (C - 1) * RH
        B_SIZE = C * RH
        EPS = 1e-05
        SSM_EPS = 1e-05

        def rat_read(res, W, gamma, beta, num_outputs):
            b, l, _ = res.shape
            x = res.reshape(b, l, H, C)
            y = jnp.einsum('blhc,hoc->bloh', x, W)
            mu = y.mean(-1, keepdims=True)
            var = y.var(-1, keepdims=True)
            yn = (y - mu) * jax.lax.rsqrt(var + EPS)
            yn = yn * gamma.reshape(num_outputs, H) + beta.reshape(num_outputs, H)
            return yn.reshape(b, l, num_outputs * H)

        def rope(x, pos):
            half = HD // 2
            inv = 1.0 / 10000.0 ** (jnp.arange(half, dtype=jnp.float32) / half)
            ang = pos.astype(jnp.float32)[..., None] * inv
            cos = jnp.cos(ang)[:, :, None, :]
            sin = jnp.sin(ang)[:, :, None, :]
            x1, x2 = (x[..., :half], x[..., half:])
            return jnp.concatenate([x1 * cos - x2 * sin, x2 * cos + x1 * sin], axis=-1)

        def attention(qkv_in, qkv_w, pos):
            b, l, _ = qkv_in.shape
            q, k, v = jnp.split(qkv_in, 3, axis=-1)
            q = jnp.einsum('bli,oi->blo', q, qkv_w[0]).reshape(b, l, NH, HD)
            k = jnp.einsum('bli,oi->blo', k, qkv_w[1]).reshape(b, l, NH, HD)
            v = jnp.einsum('bli,oi->blo', v, qkv_w[2]).reshape(b, l, NH, HD)
            q = rope(q, pos)
            k = rope(k, pos)
            scores = jnp.einsum('bqhd,bkhd->bhqk', q, k) / np.sqrt(HD).astype(np.float32)
            mask = jnp.tril(jnp.ones((l, l), dtype=bool))
            scores = jnp.where(mask, scores, jnp.float32(-1e+30))
            p = jax.nn.softmax(scores, axis=-1)
            o = jnp.einsum('bhqk,bkhd->bqhd', p, v)
            return o.reshape(b, l, H)

        def rat_write(res, y, wod_w, wab_w, wab_b, du_w, du_b):
            b, l, _ = res.shape
            o_d = y @ wod_w.T
            A_B = y @ wab_w.T + wab_b
            out = o_d[..., :H]
            delta_low = o_d[..., H:]
            A_logit = A_B[..., :A_SIZE]
            B_proj = A_B[..., A_SIZE:2 * A_SIZE]
            B_skip = A_B[..., 2 * A_SIZE:]
            delta = jax.nn.softplus(delta_low @ du_w.T + du_b)
            hs = res.reshape(b, l, HS, RH, C)
            out = out.reshape(b, l, HS, RH, 1)
            delta = delta.reshape(b, l, HS, RH, 1)
            A_logit = A_logit.reshape(b, l, 1, RH, C - 1)
            B_proj = B_proj.reshape(b, l, 1, RH, C - 1)
            B_skip = B_skip.reshape(b, l, 1, RH, 1)
            A_neg = -jax.nn.softplus(A_logit)
            A_bar = jnp.exp(delta * A_neg)
            B_bar = (A_bar - 1.0) / (A_neg - SSM_EPS) * B_proj
            B_bar_skip = delta * B_skip
            A_full = jnp.concatenate([A_bar, jnp.ones_like(A_bar[..., :1])], axis=-1)
            B_full = jnp.concatenate([B_bar, B_bar_skip], axis=-1)
            return (hs * A_full + out * B_full).reshape(b, l, H * C)

        def layer_forward(hidden_states, position_ids, attn_read_w, attn_read_g, attn_read_b, qkv_w, attn_wod_w, attn_wab_w, attn_wab_b, attn_du_w, attn_du_b, mlp_read_w, mlp_read_g, mlp_read_b, mlp_in_w, mlp_wod_w, mlp_wab_w, mlp_wab_b, mlp_du_w, mlp_du_b):
            qkv_in = rat_read(hidden_states, attn_read_w, attn_read_g, attn_read_b, 3)
            attn_out = attention(qkv_in, qkv_w, position_ids)
            hidden_states = rat_write(hidden_states, attn_out, attn_wod_w, attn_wab_w, attn_wab_b, attn_du_w, attn_du_b)
            mlp_in = rat_read(hidden_states, mlp_read_w, mlp_read_g, mlp_read_b, 2)
            g_in, u_in = (mlp_in[..., :H], mlp_in[..., H:])
            gate = jnp.einsum('bli,oi->blo', g_in, mlp_in_w[0])
            up = jnp.einsum('bli,oi->blo', u_in, mlp_in_w[1])
            mlp_out = jax.nn.silu(gate) * up
            hidden_states = rat_write(hidden_states, mlp_out, mlp_wod_w, mlp_wab_w, mlp_wab_b, mlp_du_w, mlp_du_b)
            return hidden_states
        key = jax.random.key(seed)
        ks = jax.random.split(key, 20)
        B, L = (2, 1024)
        s = 0.02
        return {'hidden_states': jax.random.normal(ks[0], (B, L, H * C), jnp.float32), 'position_ids': jnp.tile(jnp.arange(L, dtype=jnp.int64), (B, 1)), 'attn_read_w': jax.random.normal(ks[1], (H, 3, C), jnp.float32) / np.sqrt(C).astype(np.float32), 'attn_read_g': jnp.ones((3 * H,), jnp.float32), 'attn_read_b': jnp.zeros((3 * H,), jnp.float32), 'qkv_w': jax.random.normal(ks[2], (3, H, H), jnp.float32) * s, 'attn_wod_w': jax.random.normal(ks[3], (H + DR, H), jnp.float32) * s, 'attn_wab_w': jax.random.normal(ks[4], (A_SIZE + B_SIZE, H), jnp.float32) * s, 'attn_wab_b': jax.random.normal(ks[5], (A_SIZE + B_SIZE,), jnp.float32) * s, 'attn_du_w': jax.random.normal(ks[6], (H, DR), jnp.float32) * s, 'attn_du_b': jax.random.normal(ks[7], (H,), jnp.float32) * s, 'mlp_read_w': jax.random.normal(ks[8], (H, 2, C), jnp.float32) / np.sqrt(C).astype(np.float32), 'mlp_read_g': jnp.ones((2 * H,), jnp.float32), 'mlp_read_b': jnp.zeros((2 * H,), jnp.float32), 'mlp_in_w': jax.random.normal(ks[9], (2, M, H), jnp.float32) * s, 'mlp_wod_w': jax.random.normal(ks[10], (H + DR, M), jnp.float32) * s, 'mlp_wab_w': jax.random.normal(ks[11], (A_SIZE + B_SIZE, M), jnp.float32) * s, 'mlp_wab_b': jax.random.normal(ks[12], (A_SIZE + B_SIZE,), jnp.float32) * s, 'mlp_du_w': jax.random.normal(ks[13], (H, DR), jnp.float32) * s, 'mlp_du_b': jax.random.normal(ks[14], (H,), jnp.float32) * s}
    _L0_xattn_all = _L0_xattn_setup()
    _L0_xattn_in = {k: v for k, v in _L0_xattn_all.items() if k in ('attn_read_w', 'attn_read_g', 'attn_read_b', 'qkv_w', 'attn_wod_w', 'attn_wab_w', 'attn_wab_b', 'attn_du_w', 'attn_du_b', 'mlp_read_w', 'mlp_read_g', 'mlp_read_b', 'mlp_wod_w', 'mlp_wab_w', 'mlp_wab_b', 'mlp_du_w', 'mlp_du_b')}
    del _L0_xattn_all

    def _L0_ffn_setup():
        import jax, jax.numpy as jnp
        import numpy as np
        ALPHA = 32
        R = 16
        SCALING = ALPHA / R
        key = jax.random.key(seed)
        k1, k2, k3, k4 = jax.random.split(key, 4)
        B_, S, D = (4, 1024, 2048)
        H, r, O = (8, R, 2048)
        x = jax.random.normal(k1, (B_, S, D), dtype=jnp.float32)
        A = jax.random.normal(k2, (H, r, D), dtype=jnp.float32) * 0.02
        Bm = jax.random.normal(k3, (H, O, r), dtype=jnp.float32) * 0.02
        Wr = jax.random.normal(k4, (H, D), dtype=jnp.float32) * 0.02
        br = jnp.zeros((H,), dtype=jnp.float32)
        return {'x': x, 'A': A, 'B': Bm, 'Wr': Wr, 'br': br}
    _L0_ffn_all = _L0_ffn_setup()
    _L0_ffn_in = {k: v for k, v in _L0_ffn_all.items() if k in ('A', 'B', 'Wr', 'br')}
    del _L0_ffn_all
    return {'x': x, 'pos_BxS': pos_BxS, 'ctx_1024': ctx_1024, 'L0_xattn_attn_read_w': _L0_xattn_in['attn_read_w'], 'L0_xattn_attn_read_g': _L0_xattn_in['attn_read_g'], 'L0_xattn_attn_read_b': _L0_xattn_in['attn_read_b'], 'L0_xattn_qkv_w': _L0_xattn_in['qkv_w'], 'L0_xattn_attn_wod_w': _L0_xattn_in['attn_wod_w'], 'L0_xattn_attn_wab_w': _L0_xattn_in['attn_wab_w'], 'L0_xattn_attn_wab_b': _L0_xattn_in['attn_wab_b'], 'L0_xattn_attn_du_w': _L0_xattn_in['attn_du_w'], 'L0_xattn_attn_du_b': _L0_xattn_in['attn_du_b'], 'L0_xattn_mlp_read_w': _L0_xattn_in['mlp_read_w'], 'L0_xattn_mlp_read_g': _L0_xattn_in['mlp_read_g'], 'L0_xattn_mlp_read_b': _L0_xattn_in['mlp_read_b'], 'L0_xattn_mlp_wod_w': _L0_xattn_in['mlp_wod_w'], 'L0_xattn_mlp_wab_w': _L0_xattn_in['mlp_wab_w'], 'L0_xattn_mlp_wab_b': _L0_xattn_in['mlp_wab_b'], 'L0_xattn_mlp_du_w': _L0_xattn_in['mlp_du_w'], 'L0_xattn_mlp_du_b': _L0_xattn_in['mlp_du_b'], 'L0_ffn_A': _L0_ffn_in['A'], 'L0_ffn_B': _L0_ffn_in['B'], 'L0_ffn_Wr': _L0_ffn_in['Wr'], 'L0_ffn_br': _L0_ffn_in['br']}

def reference(x, pos_BxS, ctx_1024, L0_xattn_attn_read_w, L0_xattn_attn_read_g, L0_xattn_attn_read_b, L0_xattn_qkv_w, L0_xattn_attn_wod_w, L0_xattn_attn_wab_w, L0_xattn_attn_wab_b, L0_xattn_attn_du_w, L0_xattn_attn_du_b, L0_xattn_mlp_read_w, L0_xattn_mlp_read_g, L0_xattn_mlp_read_b, L0_xattn_mlp_wod_w, L0_xattn_mlp_wab_w, L0_xattn_mlp_wab_b, L0_xattn_mlp_du_w, L0_xattn_mlp_du_b, L0_ffn_A, L0_ffn_B, L0_ffn_Wr, L0_ffn_br):
    import jax
    import jax.numpy as jnp

    def _L0_xattn_ref(hidden_states, position_ids, attn_read_w, attn_read_g, attn_read_b, qkv_w, attn_wod_w, attn_wab_w, attn_wab_b, attn_du_w, attn_du_b, mlp_read_w, mlp_read_g, mlp_read_b, mlp_in_w, mlp_wod_w, mlp_wab_w, mlp_wab_b, mlp_du_w, mlp_du_b):
        import jax, jax.numpy as jnp
        import numpy as np
        H = 512
        C = 4
        RH = 16
        HS = H // RH
        DR = 8
        M = 2048
        NH = 16
        HD = H // NH
        A_SIZE = (C - 1) * RH
        B_SIZE = C * RH
        EPS = 1e-05
        SSM_EPS = 1e-05

        def rat_read(res, W, gamma, beta, num_outputs):
            b, l, _ = res.shape
            x = res.reshape(b, l, H, C)
            y = jnp.einsum('blhc,hoc->bloh', x, W)
            mu = y.mean(-1, keepdims=True)
            var = y.var(-1, keepdims=True)
            yn = (y - mu) * jax.lax.rsqrt(var + EPS)
            yn = yn * gamma.reshape(num_outputs, H) + beta.reshape(num_outputs, H)
            return yn.reshape(b, l, num_outputs * H)

        def rope(x, pos):
            half = HD // 2
            inv = 1.0 / 10000.0 ** (jnp.arange(half, dtype=jnp.float32) / half)
            ang = pos.astype(jnp.float32)[..., None] * inv
            cos = jnp.cos(ang)[:, :, None, :]
            sin = jnp.sin(ang)[:, :, None, :]
            x1, x2 = (x[..., :half], x[..., half:])
            return jnp.concatenate([x1 * cos - x2 * sin, x2 * cos + x1 * sin], axis=-1)

        def attention(qkv_in, qkv_w, pos):
            b, l, _ = qkv_in.shape
            q, k, v = jnp.split(qkv_in, 3, axis=-1)
            q = jnp.einsum('bli,oi->blo', q, qkv_w[0]).reshape(b, l, NH, HD)
            k = jnp.einsum('bli,oi->blo', k, qkv_w[1]).reshape(b, l, NH, HD)
            v = jnp.einsum('bli,oi->blo', v, qkv_w[2]).reshape(b, l, NH, HD)
            q = rope(q, pos)
            k = rope(k, pos)
            scores = jnp.einsum('bqhd,bkhd->bhqk', q, k) / np.sqrt(HD).astype(np.float32)
            mask = jnp.tril(jnp.ones((l, l), dtype=bool))
            scores = jnp.where(mask, scores, jnp.float32(-1e+30))
            p = jax.nn.softmax(scores, axis=-1)
            o = jnp.einsum('bhqk,bkhd->bqhd', p, v)
            return o.reshape(b, l, H)

        def rat_write(res, y, wod_w, wab_w, wab_b, du_w, du_b):
            b, l, _ = res.shape
            o_d = y @ wod_w.T
            A_B = y @ wab_w.T + wab_b
            out = o_d[..., :H]
            delta_low = o_d[..., H:]
            A_logit = A_B[..., :A_SIZE]
            B_proj = A_B[..., A_SIZE:2 * A_SIZE]
            B_skip = A_B[..., 2 * A_SIZE:]
            delta = jax.nn.softplus(delta_low @ du_w.T + du_b)
            hs = res.reshape(b, l, HS, RH, C)
            out = out.reshape(b, l, HS, RH, 1)
            delta = delta.reshape(b, l, HS, RH, 1)
            A_logit = A_logit.reshape(b, l, 1, RH, C - 1)
            B_proj = B_proj.reshape(b, l, 1, RH, C - 1)
            B_skip = B_skip.reshape(b, l, 1, RH, 1)
            A_neg = -jax.nn.softplus(A_logit)
            A_bar = jnp.exp(delta * A_neg)
            B_bar = (A_bar - 1.0) / (A_neg - SSM_EPS) * B_proj
            B_bar_skip = delta * B_skip
            A_full = jnp.concatenate([A_bar, jnp.ones_like(A_bar[..., :1])], axis=-1)
            B_full = jnp.concatenate([B_bar, B_bar_skip], axis=-1)
            return (hs * A_full + out * B_full).reshape(b, l, H * C)

        def layer_forward(hidden_states, position_ids, attn_read_w, attn_read_g, attn_read_b, qkv_w, attn_wod_w, attn_wab_w, attn_wab_b, attn_du_w, attn_du_b, mlp_read_w, mlp_read_g, mlp_read_b, mlp_in_w, mlp_wod_w, mlp_wab_w, mlp_wab_b, mlp_du_w, mlp_du_b):
            qkv_in = rat_read(hidden_states, attn_read_w, attn_read_g, attn_read_b, 3)
            attn_out = attention(qkv_in, qkv_w, position_ids)
            hidden_states = rat_write(hidden_states, attn_out, attn_wod_w, attn_wab_w, attn_wab_b, attn_du_w, attn_du_b)
            mlp_in = rat_read(hidden_states, mlp_read_w, mlp_read_g, mlp_read_b, 2)
            g_in, u_in = (mlp_in[..., :H], mlp_in[..., H:])
            gate = jnp.einsum('bli,oi->blo', g_in, mlp_in_w[0])
            up = jnp.einsum('bli,oi->blo', u_in, mlp_in_w[1])
            mlp_out = jax.nn.silu(gate) * up
            hidden_states = rat_write(hidden_states, mlp_out, mlp_wod_w, mlp_wab_w, mlp_wab_b, mlp_du_w, mlp_du_b)
            return hidden_states
        return layer_forward(hidden_states, position_ids, attn_read_w, attn_read_g, attn_read_b, qkv_w, attn_wod_w, attn_wab_w, attn_wab_b, attn_du_w, attn_du_b, mlp_read_w, mlp_read_g, mlp_read_b, mlp_in_w, mlp_wod_w, mlp_wab_w, mlp_wab_b, mlp_du_w, mlp_du_b)

    def _L0_ffn_ref(x, A, B, Wr, br):
        import jax, jax.numpy as jnp
        import numpy as np
        ALPHA = 32
        R = 16
        SCALING = ALPHA / R
        H = A.shape[0]
        router_logits = jnp.einsum('bsd,hd->bsh', x, Wr) + br
        scores = H * jax.nn.softmax(router_logits, axis=-1)
        low = jnp.einsum('bsd,hrd->bshr', x, A)
        out = jnp.einsum('bshr,hor,bsh->bso', low, B, scores)
        return SCALING * out
    x = x + _L0_xattn_ref(_layernorm(x, axis=-1), pos_BxS, L0_xattn_attn_read_w, L0_xattn_attn_read_g, L0_xattn_attn_read_b, L0_xattn_qkv_w, L0_xattn_attn_wod_w, L0_xattn_attn_wab_w, L0_xattn_attn_wab_b, L0_xattn_attn_du_w, L0_xattn_attn_du_b, L0_xattn_mlp_read_w, L0_xattn_mlp_read_g, L0_xattn_mlp_read_b, ctx_1024, L0_xattn_mlp_wod_w, L0_xattn_mlp_wab_w, L0_xattn_mlp_wab_b, L0_xattn_mlp_du_w, L0_xattn_mlp_du_b)
    x = x + _L0_ffn_ref(_layernorm(x, axis=-1), L0_ffn_A, L0_ffn_B, L0_ffn_Wr, L0_ffn_br)
    return x

_drawn_inputs = setup_inputs


def setup_inputs(seed=0):
    import zlib

    import numpy as np

    out = dict(_drawn_inputs(seed))
    spreads = {'L0_xattn_attn_read_g': (1.0, 0.2),
     'L0_xattn_attn_read_b': (0.0, 0.1),
     'L0_xattn_mlp_read_g': (1.0, 0.2),
     'L0_xattn_mlp_read_b': (0.0, 0.1),
     'L0_ffn_br': (0.0, 0.1)}
    factors = {}
    for name, (base, spread) in spreads.items():
        noise = np.random.default_rng([zlib.crc32(name.encode()), seed]).standard_normal(out[name].shape)
        drawn = base * np.exp(spread * noise) if base else spread * noise
        out[name] = jnp.asarray(drawn.astype(out[name].dtype))
    for name, factor in factors.items():
        out[name] = (out[name] * factor).astype(out[name].dtype)
    return out
```

```python
from contextlib import ExitStack

import numpy as np

import concourse.bass as bass
from concourse import mybir

F32 = mybir.dt.float32
F32R = mybir.dt.float32r
BF16 = mybir.dt.bfloat16
I32 = mybir.dt.int32
ALU = mybir.AluOpType
ACT = mybir.ActivationFunctionType
AX_X = mybir.AxisListType.X

P = 128
B, L, D = 2, 1024, 2048
H, C = 512, 4
NH = 16
HD = H // NH
HALF = HD // 2
RH = 16
HS = H // RH
DR = 8
M = 2048
NE, RANK = 8, 16
EPS = 1e-5
SSM_EPS = 1e-5
T = B * L
NT = T // P
TPB = L // P
BLK = 512
TB = BLK // P
NBLK = T // BLK
DCH = D // P
HCH = H // P
MCH = M // P
NA = (C - 1) * RH
GATES = 2 * NA + RH
ABW = DR + GATES
WOD = H + ABW
RD1, RD2 = 3, 2
HPC = P // C
EW = NE * RANK
NEG = -1e30


def call(op, *args, **options):
    return lambda: op(*args, **options)


class Lane:

    def __init__(self, name, engine, sem):
        self.name, self.e, self.sem, self.count, self.queue, self.seen = name, engine, sem, 0, [], {}

    def wait(self, *tickets):
        for t in tickets:
            if t is None:
                continue
            sem, value = t
            if self.seen.get(sem.name, 0) < value:
                self.seen[sem.name] = value
                self.queue.append(lambda e=self.e, s=sem, v=value: e.wait_ge(s, v))

    def do(self, make, *tickets):
        self.wait(*tickets)
        self.count += 1
        self.queue.append(lambda: make().then_inc(self.sem, 1))
        return (self.sem, self.count)

    def quiet(self, make, *tickets):
        self.wait(*tickets)
        self.queue.append(make)

    def last(self):
        return (self.sem, self.count) if self.count else None


class Flow:

    def __init__(self, sem):
        self.sem, self.count = sem, 0

    def dma(self, lane, dst, src, *tickets):
        lane.wait(*tickets)
        self.count += 16
        dst, src = (a.bitcast(F32) if a.dtype == F32R else a for a in (dst, src))
        lane.queue.append(lambda: lane.e.dma_start(dst, src).then_inc(self.sem, 16))
        return (self.sem, self.count)

    def last(self):
        return (self.sem, self.count) if self.count else None


class Banks:

    def __init__(self, banks):
        self.banks, self.turn, self.read = banks, 0, {b: None for b in banks}

    def take(self):
        b = self.banks[self.turn % len(self.banks)]
        self.turn += 1
        return b, self.read[b]


def weave(*gens):
    live = [[g, w, 0.0] for g, w in gens]
    while live:
        for item in list(live):
            item[2] += item[1]
            while item[2] >= 1 and item in live:
                item[2] -= 1
                if next(item[0], StopIteration) is StopIteration:
                    live.remove(item)


def program(nc, x, xT, pos, inv_freq, ident_in, causal_in, spread_in,
            read1_in, gamma1_in, beta1_in, qkvT, wod1T, wab1_b, du1T, du1_b,
            read2_in, gamma2_in, beta2_in, mlp_inT, wod2T, wab2_b, du2T, du2_b,
            expA, expB, br, out):
    with ExitStack() as ctx:
        sems = {}

        def sem(name):
            sems[name] = ctx.enter_context(nc.semaphore(name))
            return sems[name]

        pe = Lane("pe", nc.tensor, sem("pe_done"))
        act = Lane("act", nc.scalar, sem("act_done"))
        dve = Lane("dve", nc.vector, sem("dve_done"))
        pool = Lane("pool", nc.gpsimd, sem("pool_done"))
        sp = Lane("sp", nc.sync, None)
        flows = {}

        def flow(name):
            if name not in flows:
                flows[name] = Flow(sem("dma_" + name))
            return flows[name]

        ps = ctx.enter_context(nc.psum_tensor("ps", [P, 8, 512], F32))

        def dram(name, shape, dt=F32):
            return nc.dram_tensor(name, shape, dt, kind="Internal").ap()

        rope_d = dram("rope_tables", [2, HALF, T])
        qk_d = dram("qk_split", [B, 2, NH, 2, 2, HALF, L])
        oT_d = dram("attention_out", [NT, P, HCH, P])
        win_d = dram("mlp_in_split", [2 * MCH, P, 2, HCH * P])
        hs_d = dram("hidden_after_attention", [NT, P, D])
        x2_d = dram("x_after_layer", [NT, P, D])
        v_d = dram("values", [B, P, TPB, H])

        base = (nc.sbuf_base + 31) // 32 * 32
        top = nc.sbuf_usable_end
        place = [base]

        def sb(name, shape, dt=F32):
            size = int(np.prod(shape[1:])) * (2 if dt == BF16 else 4)
            size = (size + 31) // 32 * 32
            assert place[0] + size <= top, (name, place[0] + size - top)
            t = nc.alloc_sbuf_tensor_at(name, shape, dt, offset=place[0])
            place[0] += size
            return t

        def barrier():
            done = [l.last() for l in (pe, act, dve, pool)] + [f.last() for f in flows.values()]
            for l in (pe, act, dve, pool, sp):
                l.wait(*done)

        ident = sb("ident", [P, P])
        identb = sb("identb", [P, P], BF16)
        causalb = sb("causalb", [P, P], BF16)
        mhalf = sb("mhalf", [P, 4])
        rstd1 = sb("rstd1", [P, NT])
        negm1 = sb("negm1", [P, NT])
        nmr1 = sb("nmr1", [P, NT])
        keep = place[0]

        c_ident = flow("ident").dma(sp, ident[:, :], ident_in)
        c_mhalf = pool.do(call(nc.gpsimd.memset, mhalf[:, :], -0.5))
        act.queue.append(call(nc.scalar.preload_act_table_set, "natural_log_exp_and_others"))

        def power_mhalf(dst, src, *tickets):
            n = dst.shape[1]
            return pool.do(call(nc.gpsimd.tensor_tensor, dst, src, mhalf[:, 0:n], ALU.pow), c_mhalf, *tickets)

        def project(b):
            place[0] = keep
            tag = f"p{b}_"
            wq = sb(tag + "wqkv", [P, 3 * HCH, H])
            readw = sb(tag + "read1", [P, DCH, RD1, HPC])
            wsum = sb(tag + "read1_sum", [P, DCH * RD1 * HPC])
            gam = sb(tag + "gamma1", [P, RD1 * HCH])
            bet = sb(tag + "beta1", [P, RD1 * HCH])
            cosT = sb(tag + "cos", [P, L])
            sinT = sb(tag + "sin", [P, L])
            XR, XTR, ZR, YR = 2, 2, 2, 6
            xt = [sb(tag + f"x{i}", [P, D]) for i in range(XR)]
            xTt = [sb(tag + f"xT{i}", [P, DCH, P]) for i in range(XTR)]
            zt = [sb(tag + f"z{i}", [P, DCH, RD1, HPC]) for i in range(ZR)]
            yn = [sb(tag + f"y{i}", [P, RD1, H]) for i in range(YR)]
            yT = sb(tag + "yT", [P, RD1 * HCH, BLK])
            rt = sb(tag + "rope", [P, 2, 4, BLK])
            hi = sb(tag + "rope_hi", [P, 2, 2, BLK], F32R)
            lo = sb(tag + "rope_lo", [P, 2, 2, BLK], F32R)
            vt = sb(tag + "v", [P, TPB, H])
            st = sb(tag + "stats", [P, 2, 4, 6])
            mv = sb(tag + "moments", [P, 2, 8])
            sy = sb(tag + "ystats", [P, 2, RD1, 6])
            my = sb(tag + "ymoments", [P, 2, RD1, 2])
            sc = sb(tag + "yscale", [P, 2, 4, RD1])

            f = flow("p_const")
            f.dma(sp, gam[:, :], gamma1_in)
            f.dma(sp, bet[:, :], beta1_in)
            first = b == 0

            spread = sb(tag + "spread", [P, HPC])
            wrep = sb(tag + "read1_rep", [P, DCH * RD1])
            ones = sb(tag + "ones", [P, P])
            f.dma(sp, spread[:, :], spread_in)
            c_rep = f.dma(sp, wrep[:, :], read1_in)
            c_ones = pool.do(call(nc.gpsimd.memset, ones[:, :], 1.0))
            flat = readw[:, :, :, :].rearrange("p a b c -> p (a b) c")
            n48 = DCH * RD1
            t_read = dve.do(call(nc.vector.tensor_tensor,
                flat, wrep[:, :].unsqueeze(2).broadcast_to([P, n48, HPC]),
                spread[:, :].unsqueeze(1).broadcast_to([P, n48, HPC]), ALU.mult), c_rep)
            flat1 = readw[:, :, :, :].rearrange("p a b c -> p (a b c)")
            for n in range(3):
                t_sum = pe.do(call(nc.tensor.matmul, ps[:, n, :], ones[:, :], flat1[:, 512 * n:512 * n + 512],
                                                           start=True, stop=True), t_read, c_ones)
            t_wsum = dve.do(call(nc.vector.tensor_copy,
                wsum[:, :], ps[:, 0:3, :].rearrange("p a b -> p (a b)")), t_sum)

            if first:
                cf = sb(tag + "causal_f32", [P, P])
                c_causal = flow("causal").dma(sp, cf[:, :], causal_in)
                dve.do(call(nc.vector.tensor_copy, identb[:, :], ident[:, :]), c_ident)
                dve.do(call(nc.vector.tensor_copy, causalb[:, :], cf[:, :]), c_causal)
                NB8 = P // HALF
                W8 = T // NB8
                posi = sb(tag + "pos_i", [P, W8], I32)
                ang = sb(tag + "angle", [P, W8])
                kk = sb(tag + "turns", [P, W8])
                sn = sb(tag + "sine", [P, 2, W8])
                invf = sb(tag + "inv_freq", [P, 1])
                g = flow("rope_in")
                g.dma(sp, invf[:, :], inv_freq)
                for k in range(NB8):
                    t_pos = g.dma(sp, posi[HALF * k:HALF * k + HALF, :],
                                  pos[k * W8:(k + 1) * W8].unsqueeze(0).broadcast_to([HALF, W8]))
                TWO_PI = 2 * np.pi
                C1 = 6.28125
                C2 = float(np.float32(np.floor((TWO_PI - C1) * 2 ** 21) / 2 ** 21))
                C3 = float(np.float32(TWO_PI - C1 - C2))
                MAGIC = 1.5 * 2 ** 23
                V = nc.vector
                d = dve.do(call(V.tensor_copy, ang[:, :], posi[:, :]), t_pos)
                d = dve.do(call(V.tensor_scalar, ang[:, :], ang[:, :], invf[:, 0:1], None, ALU.mult), d)
                d = dve.do(call(V.tensor_scalar, kk[:, :], ang[:, :], 1.0 / TWO_PI, MAGIC, ALU.mult, ALU.add), d)
                d = dve.do(call(V.tensor_scalar, kk[:, :], kk[:, :], MAGIC, None, ALU.subtract), d)
                for cc in (C1, C2, C3):
                    d = dve.do(call(V.scalar_tensor_tensor,
                        out=ang[:, :], in0=kk[:, :], scalar=-cc, in1=ang[:, :], op0=ALU.mult, op1=ALU.add), d)
                PI = 3.1415925
                d = dve.do(call(V.tensor_scalar, sn[:, 0, :], ang[:, :], float(np.pi / 2), None, ALU.add), d)
                d = dve.do(call(V.tensor_scalar, kk[:, :], sn[:, 0, :], PI, -TWO_PI, ALU.is_gt, ALU.mult), d)
                d = dve.do(call(V.tensor_tensor, sn[:, 0, :], sn[:, 0, :], kk[:, :], ALU.add), d)
                d = dve.do(call(V.tensor_scalar, sn[:, 0, :], sn[:, 0, :], PI, -PI, ALU.min, ALU.max), d)
                d = dve.do(call(V.tensor_scalar, sn[:, 1, :], ang[:, :], PI, -PI, ALU.min, ALU.max), d)
                a = act.do(call(nc.scalar.activation, sn[:, :, :], sn[:, :, :], ACT.Sin), d)
                act.queue.append(call(nc.scalar.preload_act_table_set, "natural_log_exp_and_others"))
                for k in range(NB8):
                    for w in range(2):
                        t_rope = flow("rope_out").dma(sp, rope_d[w, :, k * W8:(k + 1) * W8], sn[HALF * k:HALF * k + HALF, w, :], a)
            else:
                t_rope = None
            g = flow("rope_tab")
            for k in range(P // HALF):
                for w, tab in enumerate((cosT, sinT)):
                    t_tab = g.dma(sp, tab[HALF * k:HALF * k + HALF, :], rope_d[w, :, b * L:(b + 1) * L], t_rope)
            t_w = flow("wqkv").dma(sp, wq[:, :, :], qkvT)
            t_qs = dve.do(call(nc.vector.tensor_scalar, wq[:, 0:HCH, :], wq[:, 0:HCH, :],
                                                          float(1.0 / np.float32(np.sqrt(HD))), None, ALU.mult), t_w)

            x_read, xT_read, z_read = {}, {}, {}
            y_read = t_wsum
            y_ready, y_turned = {}, {}

            def load(i):
                n = b * TPB + i
                a = flow(f"x{i % XR}").dma(sp, xt[i % XR][:, :], x[n], x_read.get(i - XR))
                c = flow(f"xT{i % XTR}").dma(sp, xTt[i % XTR][:, :, :], xT[n], xT_read.get(i - XTR))
                return a, c

            loaded = {0: load(0), 1: load(1)}

            def read(i):
                nonlocal y_read
                n = b * TPB + i
                s = i % 2
                lx, lxT = loaded.pop(i)
                V = nc.vector
                for q in range(4):
                    d = dve.do(call(V.bn_stats, st[:, s, q, :], xt[i % XR][:, 512 * q:512 * q + 512]), lx)
                x_read[i] = d
                d = dve.do(call(V.bn_aggr, mv[:, s, 0:2], st[:, s, :, :]), d)
                d = dve.do(call(V.tensor_scalar, negm1[:, n:n + 1], mv[:, s, 0:1], -1.0, None, ALU.mult), d)
                d = dve.do(call(V.tensor_scalar, mv[:, s, 2:3], mv[:, s, 1:2], EPS, None, ALU.add), d)
                g = power_mhalf(rstd1[:, n:n + 1], mv[:, s, 2:3], d)
                zw = RD1 * HPC
                for j in range(DCH):
                    mk = call(nc.tensor.matmul,
                        ps[:, j // 4, zw * (j % 4):zw * (j % 4) + zw], xTt[i % XTR][:, j, :],
                        readw[:, j, :, :].rearrange("p a b -> p (a b)"), start=True, stop=True)
                    if j < DCH - 1:
                        pe.quiet(mk, lxT, t_read, y_read)
                    else:
                        t = pe.do(mk)
                xT_read[i] = t
                if i + 2 < TPB:
                    loaded[i + 2] = load(i + 2)
                yield
                z = zt[i % ZR]
                d = dve.do(call(V.scalar_tensor_tensor,
                    out=z[:, :, :, :].rearrange("p (k a) b c -> p k (a b c)", k=4),
                    in0=wsum[:, :].rearrange("p (k n) -> p k n", k=4),
                    scalar=negm1[:, n:n + 1], in1=ps[:, 0:4, 0:4 * zw], op0=ALU.mult, op1=ALU.add),
                    t, t_wsum, z_read.get(i - ZR), d)
                y_read = d
                for o in range(RD1):
                    e = dve.do(call(V.bn_stats, sy[:, s, o, :], z[:, :, o, :]), d)
                for o in range(RD1):
                    e2 = dve.do(call(V.bn_aggr, my[:, s, o, :], sy[:, s, o, :]), e)
                e = dve.do(call(V.tensor_tensor, mv[:, s, 3:4], rstd1[:, n:n + 1], rstd1[:, n:n + 1], ALU.mult), g)
                dve.do(call(V.tensor_tensor, nmr1[:, n:n + 1], rstd1[:, n:n + 1], negm1[:, n:n + 1], ALU.mult), g)
                e = dve.do(call(V.tensor_scalar, sc[:, s, 0, :], my[:, s, :, 1], mv[:, s, 3:4], EPS,
                                                   ALU.mult, ALU.add), e, e2)
                g = power_mhalf(sc[:, s, 1, :], sc[:, s, 0, :], e)
                e = dve.do(call(V.tensor_scalar, sc[:, s, 2, :], sc[:, s, 1, :], rstd1[:, n:n + 1], None,
                                                   ALU.mult), g)
                e = dve.do(call(V.scalar_tensor_tensor,
                    out=sc[:, s, 3, :], in0=my[:, s, :, 0], scalar=-1.0, in1=sc[:, s, 2, :],
                    op0=ALU.mult, op1=ALU.mult), e)
                for o in range(RD1):
                    a = act.do(call(nc.scalar.activation,
                        yn[i % YR][:, o, :].rearrange("p (a b) -> p a b", b=HPC), z[:, :, o, :], ACT.Identity,
                        bias=sc[:, s, 3, o:o + 1], scale=sc[:, s, 2, o:o + 1]), e, y_turned.get(i - YR))
                z_read[i] = y_ready[i] = a
                yield

            ring = Banks([4, 5, 6, 7])
            yT_read = [None]

            def reads(blk):
                for i in range(blk * TB, blk * TB + TB):
                    yield from read(i)

            def turn(blk):
                ready = []
                for k in range(RD1 * HCH):
                    o, hc = divmod(k, HCH)
                    bank, free = ring.take()
                    for q in range(TB):
                        i = blk * TB + q
                        mk = call(nc.tensor.transpose,
                            ps[:, bank, P * q:P * q + P], yn[i % YR][:, o, P * hc:P * hc + P], ident[:, :])
                        if q < TB - 1:
                            pe.quiet(mk, y_ready[i], free, c_ident)
                        else:
                            t = pe.do(mk, y_ready[i])
                    if k % 2:
                        r = dve.do(call(nc.vector.tensor_scalar,
                            yT[:, k, :], ps[:, bank, :], gam[:, k:k + 1], bet[:, k:k + 1], ALU.mult, ALU.add),
                            t, yT_read[0], c_rep)
                    else:
                        r = act.do(call(nc.scalar.activation,
                            yT[:, k, :], ps[:, bank, :], ACT.Identity, bias=bet[:, k:k + 1],
                            scale=gam[:, k:k + 1]), t, yT_read[0], c_rep)
                    ring.read[bank] = r
                    ready.append(r)
                    yield
                for q in range(TB):
                    y_turned[blk * TB + q] = t
                yT_ready[blk] = ready

            yT_ready = {}
            split_stored = {0: None, 1: None}
            qk_stored = []

            def qkv(blk):
                ready = yT_ready[blk]
                t0 = blk * BLK
                for pair in range(4):
                    w, oc = divmod(pair, 2)
                    s = pair % 2
                    got = []
                    for half in range(2):
                        bank, free = ring.take()
                        col = (half * 2 + oc) * P
                        for ic in range(HCH):
                            mk = call(nc.tensor.matmul,
                                ps[:, bank, :], wq[:, w * HCH + ic, col:col + P], yT[:, w * HCH + ic, :],
                                start=(ic == 0), stop=(ic == HCH - 1))
                            if ic < HCH - 1:
                                pe.quiet(mk, free, t_qs, ready[w * HCH + ic])
                            else:
                                t = pe.do(mk, ready[w * HCH + ic])
                        got.append((bank, t))
                        yield
                    V = nc.vector
                    cs, sn_ = cosT[:, t0:t0 + BLK], sinT[:, t0:t0 + BLK]
                    (b1, p1), (b2, p2) = got
                    dve.do(call(V.tensor_tensor, rt[:, s, 0, :], ps[:, b1, :], cs, ALU.mult), p1, t_tab, rt_read[s])
                    r1 = dve.do(call(V.tensor_tensor, rt[:, s, 3, :], ps[:, b1, :], sn_, ALU.mult))
                    dve.do(call(V.tensor_tensor, rt[:, s, 1, :], ps[:, b2, :], sn_, ALU.mult), p2)
                    r2 = dve.do(call(V.tensor_tensor, rt[:, s, 2, :], ps[:, b2, :], cs, ALU.mult))
                    ring.read[b1], ring.read[b2] = r1, r2
                    G = nc.gpsimd
                    ga = pool.do(call(G.tensor_tensor, rt[:, s, 0, :], rt[:, s, 0, :], rt[:, s, 1, :],
                                                         ALU.subtract), r2)
                    gb = pool.do(call(G.tensor_tensor, rt[:, s, 2, :], rt[:, s, 2, :], rt[:, s, 3, :], ALU.add))
                    for h_, slot, gt in ((0, 0, ga), (1, 2, gb)):
                        ah = act.do(call(nc.scalar.activation,
                            hi[:, s, h_, :], rt[:, s, slot, :], ACT.Copy), gt, split_stored[s])
                        gl = pool.do(call(G.tensor_tensor,
                            lo[:, s, h_, :], rt[:, s, slot, :], hi[:, s, h_, :].bitcast(F32), ALU.subtract), ah)
                        for hl, buf, tt in ((0, hi, ah), (1, lo, gl)):
                            stt = flow(f"split{s}").dma(
                                sp, qk_d[b, w, 8 * oc:8 * oc + 8, hl, h_, :, t0:t0 + BLK], buf[:, s, h_, :], tt)
                    rt_read[s] = gl
                    split_stored[s] = stt
                    yield
                for q in range(TB):
                    bank, free = ring.take()
                    for ic in range(HCH):
                        mk = call(nc.tensor.matmul,
                            ps[:, bank, :], yT[:, 2 * HCH + ic, P * q:P * q + P], wq[:, 2 * HCH + ic, :],
                            start=(ic == 0), stop=(ic == HCH - 1))
                        if ic < HCH - 1:
                            pe.quiet(mk, free, t_w, ready[2 * HCH + ic])
                        else:
                            t = pe.do(mk, ready[2 * HCH + ic])
                    ring.read[bank] = act.do(call(nc.scalar.activation,
                        vt[:, blk * TB + q, :], ps[:, bank, :], ACT.Copy), t)
                    yield
                yT_read[0] = t

            rt_read = {0: None, 1: None}
            nb = L // BLK
            weave((reads(0), 1))
            weave((turn(0), 1))
            for blk in range(nb):
                if blk + 1 < nb:
                    weave((qkv(blk), 2), (reads(blk + 1), 1))
                    weave((turn(blk + 1), 1))
                else:
                    weave((qkv(blk), 1))
            v_ready = act.last()
            t_v = flow("v_store").dma(sp, v_d[b], vt[:, :, :], v_ready)
            return t_v



        def attend(b, extra):
            place[0] = keep
            tag = f"a{b}_"
            NS = 8
            qs = [sb(tag + f"q{i}", [P, L], F32R) for i in range(NS)]
            ks = [sb(tag + f"k{i}", [P, L], F32R) for i in range(NS)]
            vt = sb(tag + "v", [P, TPB, H])
            PR = 2
            pt = [sb(tag + f"p{i}", [P, L]) for i in range(PR)]
            pT = [sb(tag + f"pT{g}", [P, 4, (g + 1) * TB, BLK]) for g in range(2)]
            negmax = sb(tag + "negmax", [P, 4])
            rsum = sb(tag + "rowsum", [P, 2, 4 * TB])
            rinv = sb(tag + "rowinv", [P, 4 * TB])
            rb = sb(tag + "rowinv_wide", [P, 4 * TB, HD])
            rT = sb(tag + "rowinv_T", [P, BLK])
            oT = [sb(tag + f"oT{i}", [P, BLK]) for i in range(2)]
            aux = extra(tag) if extra else None

            t_v = flow("v_load").dma(sp, vt[:, :, :], v_d[b])
            head_loaded, head_read = {}, {}

            def load_head(h):
                s = h % NS
                f = flow(f"head{s}")
                src_q = qk_d[b, 0, h].rearrange("a c r t -> (a c r) t")
                src_k = qk_d[b, 1, h].rearrange("a c r t -> a (c r) t")
                free = head_read.get(h - NS)
                for r in range(2):
                    f.dma(sp, qs[s][64 * r:64 * r + 64, :], src_q, free)
                for r in range(4):
                    t = f.dma(sp, ks[s][32 * r:32 * r + 32, :], src_k[r // 2])
                head_loaded[h] = t

            for h in range(4):
                load_head(h)
            groups = [(h4, g) for h4 in range(NH // 4) for g in range(2)]
            tiles = [(gi, h4, g, hh, q) for gi, (h4, g) in enumerate(groups) for hh in range(4) for q in range(TB)]
            SB = [0, 2]
            turned = Banks([4, 5])
            scores_read, exp_done, p_read = {}, {}, {}
            pT_ready, pT_read = {}, {0: None, 1: None}
            load = {"act": 0.0, "dve": 0.0}

            def flat(bank):
                return ps[:, bank:bank + 2, :].rearrange("p a b -> p (a b)")

            def scores(n):
                gi, h4, g, hh, q = tiles[n]
                h, qt = 4 * h4 + hh, g * TB + q
                s, bank = h % NS, SB[n % 2]
                klen = (qt + 1) * P
                for k0 in range(0, klen, 512):
                    kn = min(512, klen - k0)
                    diag = k0 + kn == klen
                    mk = call(nc.tensor.matmul,
                        ps[:, bank + k0 // 512, 0:kn], qs[s][:, qt * P:qt * P + P], ks[s][:, k0:k0 + kn],
                        start=True, stop=not diag)
                    pe.quiet(mk, head_loaded[h], scores_read.get(n - 2))
                t = pe.do(call(nc.tensor.matmul,
                    ps[:, bank + (klen - 1) // 512, (klen - P) % 512:(klen - P) % 512 + P],
                    identb[:, :], causalb[:, :], start=False, stop=True))
                if g == 1 and q == TB - 1:
                    head_read[h] = t
                d = dve.do(call(nc.vector.tensor_reduce,
                    negmax[:, n % 4:n % 4 + 1], flat(bank)[:, 0:klen], AX_X, ALU.max, negate=True), t,
                    exp_done.get(n - 4))
                col = q * 4 + hh
                a = act.do(call(nc.scalar.activation,
                    pt[n % PR][:, 0:klen], flat(bank)[:, 0:klen], ACT.Exp, bias=negmax[:, n % 4:n % 4 + 1],
                    accum_out=rsum[:, gi % 2, col:col + 1]), d, p_read.get(n - PR), sum_read.get(gi - 2))
                exp_done[n] = scores_read[n] = a
                load["dve"] += klen / .96 + 80
                load["act"] += klen / 1.2 + 280

            sum_read = {}

            def turn(n):
                gi, h4, g, hh, q = tiles[n]
                nk = g * TB + q + 1
                for k0 in range(0, nk, 4):
                    kn = min(4, nk - k0)
                    bank, free = turned.take()
                    for k in range(kn):
                        mk = call(nc.tensor.transpose,
                            ps[:, bank, P * k:P * k + P], pt[n % PR][:, P * (k0 + k):P * (k0 + k) + P], ident[:, :])
                        if k < kn - 1:
                            pe.quiet(mk, exp_done[n], free)
                        else:
                            t = pe.do(mk, exp_done[n], free)
                    dst = pT[g][:, hh, k0:k0 + kn, P * q:P * q + P]
                    src = ps[:, bank, 0:P * kn].rearrange("p (a b) -> p a b", a=kn)
                    free = pT_read[g]
                    if load["act"] < load["dve"]:
                        r = act.do(call(nc.scalar.activation, dst, src, ACT.Copy), t, free)
                        load["act"] += kn * P / 1.2 + 90
                        pT_ready.setdefault(gi, {})["act"] = r
                    else:
                        r = dve.do(call(nc.vector.tensor_copy, dst, src), t, free)
                        load["dve"] += kn * P / .96 + 80
                        pT_ready.setdefault(gi, {})["dve"] = r
                    turned.read[bank] = r
                p_read[n] = t

            o_read = {"o": None, "r": None}
            oT_stored = {}
            last_exp = {}

            def values(gi):
                h4, g = groups[gi]
                d = dve.do(call(nc.vector.reciprocal, rinv[:, :], rsum[:, gi % 2, :]), last_exp[gi])
                sum_read[gi] = d
                d = dve.do(call(nc.vector.tensor_copy,
                    rb[:, :, :], rinv[:, :].unsqueeze(2).broadcast_to([P, 4 * TB, HD])), d, o_read.get("rb"))
                for q in range(TB):
                    t = pe.do(call(nc.tensor.transpose,
                        ps[:, 7, P * q:P * q + P], rb[:, 4 * q:4 * q + 4, :].rearrange("p a b -> p (a b)"),
                        ident[:, :]), d, o_read["r"])
                o_read["rb"] = t
                a = act.do(call(nc.scalar.activation, rT[:, :], ps[:, 7, :], ACT.Copy), t, o_read["o"])
                o_read["r"] = a
                nk = (g + 1) * TB
                for k in range(nk):
                    q0 = max(0, k * P - g * BLK)
                    for hh in range(4):
                        h = 4 * h4 + hh
                        mk = call(nc.tensor.matmul,
                            ps[32 * hh:32 * hh + 32, 6, q0:BLK], vt[:, k, HD * h:HD * h + HD],
                            pT[g][:, hh, k, q0:BLK], start=(k == 0), stop=(k == nk - 1))
                        w = list(pT_ready[gi].values()) + [t_v, o_read["o"]]
                        if k == nk - 1 and hh == 3:
                            t = pe.do(mk, *w)
                        else:
                            pe.quiet(mk, *w)
                pT_read[g] = t
                s = gi % 2
                d = dve.do(call(nc.vector.tensor_tensor, oT[s][:, :], ps[:, 6, :], rT[:, :], ALU.mult),
                           t, a, oT_stored.get(gi - 2))
                o_read["o"] = d
                i0 = b * TPB + g * TB
                for q in range(TB):
                    oT_stored[gi] = flow(f"oT{s}").dma(sp, oT_d[i0 + q, :, h4, :], oT[s][:, P * q:P * q + P], d)

            per = 4 * TB
            scores(0)
            scores(1)
            for n in range(len(tiles)):
                gi = n // per
                if n % (2 * per) == 2 and gi // 2 + 1 < NH // 4:
                    for h in range(4):
                        load_head(4 * (gi // 2 + 1) + h)
                turn(n)
                if n % per == per - 1:
                    last_exp[gi] = exp_done[n]
                if n + 2 < len(tiles):
                    scores(n + 2)
                if n % per == 1 and gi:
                    values(gi - 1)
                if aux and n % 3 == 0:
                    next(aux, None)
            if aux:
                for _ in aux:
                    pass
            values(len(groups) - 1)

        def split_mlp_in(tag):
            raw = [sb(tag + f"w_raw{i}", [P, HCH * P]) for i in range(2)]
            two = [sb(tag + f"w_two{i}", [P, 2, HCH * P], F32R) for i in range(2)]

            def steps():
                done, stored = {}, {}
                for u in range(2 * MCH):
                    s = u % 2
                    l = flow(f"w_raw{s}").dma(sp, raw[s][:, :], mlp_inT[u], done.get(u - 2))
                    g = pool.do(call(nc.gpsimd.tensor_scalar,
                        two[s][:, 0, :], raw[s][:, :], 1.0, None, ALU.mult), l, stored.get(u - 2))
                    g = pool.do(call(nc.gpsimd.tensor_tensor,
                        two[s][:, 1, :], raw[s][:, :], two[s][:, 0, :].bitcast(F32), ALU.subtract), g)
                    done[u] = g
                    yield
                    stored[u] = flow(f"w_two{s}").dma(sp, win_d[u], two[s][:, :, :], g)
            return steps()

        def mix():
            place[0] = keep
            gates_b, duT, dlT = [], [], []
            f = flow("m_const")
            wod1 = sb("m_wod1", [P, HCH, WOD])
            read2 = sb("m_read2", [P, DCH + 1, RD2, HPC])
            gam = sb("m_gamma2", [P, RD2 * HCH])
            bet = sb("m_beta2", [P, RD2 * HCH])
            for k, (wab, duw, dub) in enumerate(((wab1_b, du1T, du1_b), (wab2_b, du2T, du2_b))):
                gates_b.append(sb(f"m_gate_bias{k}", [P, ABW]))
                duT.append(sb(f"m_duT{k}", [P, H]))
                dlT.append(sb(f"m_lowT{k}", [P, P]))
            hs = [sb(f"m_hs{k}", [P, D]) for k in range(2)]
            xt = sb("m_x", [P, D])
            oTt = sb("m_oT", [P, HCH, P])
            tT = [sb(f"m_hsT{k}", [P, 4, P]) for k in range(4)]
            Ab = [sb(f"m_A{k}", [P, NA * HS]) for k in range(2)]
            Qb = sb("m_Q", [P, NA * HS])
            outs2 = [sb(f"m_mlp_out{k}", [P, H]) for k in range(TB)]
            ab2 = [sb(f"m_mlp_ab{k}", [P, ABW]) for k in range(TB)]
            delta = [sb(f"m_delta{k}", [P, H]) for k in range(2)]
            outs1 = sb("m_att_out", [P, H])
            ab1 = sb("m_att_ab", [P, ABW])
            tmp = [sb(f"m_tmp{k}", [P, H]) for k in range(2)]
            g1 = [sb(f"m_gate{k}", [P, 4, NA]) for k in range(2)]
            y2 = [sb(f"m_y{k}", [P, RD2, H]) for k in range(TB)]
            st = sb("m_stats", [P, RD2, 2, 6])
            my = sb("m_moments", [P, RD2, 2])
            sc = sb("m_scale", [P, 3, RD2])
            yraw = [sb(f"m_yraw{k}", [P, BLK]) for k in range(2)]
            yhi = sb("m_yhi", [P, RD2 * HCH, BLK], F32R)
            ylo = sb("m_ylo", [P, RD2 * HCH, BLK], F32R)
            WR = 4
            win = [sb(f"m_win{k}", [P, 2, HCH, P], F32R) for k in range(WR)]
            silu = [sb(f"m_silu{k}", [P, BLK]) for k in range(2)]
            hT = sb("m_hT", [P, MCH, BLK])
            W2R = 3
            w2 = [sb(f"m_wod2_{k}", [P, WOD]) for k in range(W2R)]
            wrep = yraw[0][:, 0:DCH * RD2]
            spread = yraw[0][:, 64:64 + HPC]

            t_wod1 = f.dma(sp, wod1[:, :, :], wod1T)
            f.dma(sp, gam[:, :], gamma2_in)
            f.dma(sp, bet[:, :], beta2_in)
            flow("m_read2").dma(sp, spread, spread_in)
            t_rep = flow("m_read2").dma(sp, wrep, read2_in)
            t_z = []
            for k, (wab, duw, dub) in enumerate(((wab1_b, du1T, du1_b), (wab2_b, du2T, du2_b))):
                a = pool.do(call(nc.gpsimd.memset, duT[k][:, :], 0.0))
                c = pool.do(call(nc.gpsimd.memset, dlT[k][:, :], 0.0))
                c = pool.do(call(nc.gpsimd.memset, dlT[k][32:33, :], 1.0), c)
                d = pool.do(call(nc.gpsimd.memset, gates_b[k][:, 0:DR], 0.0), c)
                f.dma(sp, duT[k][0:DR, :], duw, a)
                f.dma(sp, duT[k][32:33, :], dub.unsqueeze(0))
                t_c = f.dma(sp, gates_b[k][:, DR:ABW], wab.unsqueeze(0).broadcast_to([P, GATES]))
                t_z += [c, d]
            n32 = DCH * RD2
            z0 = pool.do(call(nc.gpsimd.memset, read2[:, DCH, :, :], 0.0))
            t_read2 = dve.do(call(nc.vector.tensor_tensor,
                read2[:, 0:DCH, :, :].rearrange("p a b c -> p (a b) c"),
                wrep.unsqueeze(2).broadcast_to([P, n32, HPC]),
                spread.unsqueeze(1).broadcast_to([P, n32, HPC]), ALU.mult), t_rep)

            mlp_banks = Banks([0, 1, 2, 3])
            one = Banks([6, 7])
            pair_read = [None]
            V, S, G = nc.vector, nc.scalar, nc.gpsimd

            used = {}

            def write(k, out_t, ab_t, out_ready, ab_ready, hs_ready, tail):
                bank, free = one.take()
                t = pe.do(call(nc.tensor.transpose, ps[0:DR, bank, 0:P], ab_t[:, 0:DR], ident[:, :]), ab_ready, free)
                dl = dve.do(call(V.tensor_copy, dlT[k][0:DR, :], ps[0:DR, bank, 0:P]), t, used.get(("dlT", k)), *t_z)
                one.read[bank] = dl
                al = ab_t[:, DR:DR + NA]
                g = g1[k]
                a = act.do(call(S.activation, g[:, 0, :], al, ACT.Abs), ab_ready, used.get(("gate", k)))
                a = act.do(call(S.activation, g[:, 0, :], g[:, 0, :], ACT.Exp, scale=-1.0), a)
                a = act.do(call(S.activation, g[:, 0, :], g[:, 0, :], ACT.Ln, bias=1.0), a)
                d_sp = dve.do(call(V.scalar_tensor_tensor, out=g[:, 1, :], in0=al, scalar=0.0, in1=g[:, 0, :],
                                                             op0=ALU.max, op1=ALU.add), a, used.get(("gate_sp", k)))
                d = dve.do(call(V.tensor_scalar, g[:, 2, :], g[:, 1, :], -1.0, -SSM_EPS, ALU.mult, ALU.add), d_sp)
                d = dve.do(call(V.reciprocal, g[:, 3, :], g[:, 2, :]), d)
                d_gain = dve.do(call(V.tensor_tensor, g[:, 2, :], g[:, 3, :], ab_t[:, DR + NA:DR + 2 * NA],
                                                        ALU.mult), d)
                yield
                bank, free = one.take()
                t = pe.do(call(nc.tensor.matmul, ps[:, bank, :], dlT[k][:, :], duT[k][:, :], start=True, stop=True),
                          dl, free, t_c)
                used[("dlT", k)] = t
                a = act.do(call(S.activation, tmp[k][:, :], ps[:, bank, :], ACT.Abs), t, used.get(("tmp", k)))
                a = act.do(call(S.activation, tmp[k][:, :], tmp[k][:, :], ACT.Exp, scale=-1.0), a)
                a = act.do(call(S.activation, tmp[k][:, :], tmp[k][:, :], ACT.Ln, bias=1.0), a)
                d_delta = dve.do(call(V.scalar_tensor_tensor,
                    out=delta[k][:, :], in0=ps[:, bank, :], scalar=0.0, in1=tmp[k][:, :],
                    op0=ALU.max, op1=ALU.add), a, used.get(("delta", k)))
                one.read[bank] = d_delta
                A3 = Ab[k][:, :].rearrange("p (s r c) -> p s r c", s=HS, r=RH)
                A2 = Ab[k][:, :].rearrange("p (s n) -> p s n", s=HS)
                Ah = Ab[k][:, :].rearrange("p (h c) -> p h c", c=C - 1)
                Qs = Qb[:, :].rearrange("p (s n) -> p s n", s=HS)
                Qh = Qb[:, :].rearrange("p (h c) -> p h c", c=C - 1)
                dl3 = delta[k][:, :].rearrange("p (s r) -> p s r", s=HS).unsqueeze(3).broadcast_to([P, HS, RH, C - 1])
                sp3 = g[:, 1, :].rearrange("p (r c) -> p r c", r=RH).unsqueeze(1).broadcast_to([P, HS, RH, C - 1])
                gp = pool.do(call(G.tensor_tensor, A3, dl3, sp3, ALU.mult), d_delta, d_sp, used.get(("A", k)))
                used[("gate_sp", k)] = gp
                a_A = act.do(call(S.activation, Ab[k][:, :], Ab[k][:, :], ACT.Exp, scale=-1.0), gp)
                bs = ab_t[:, DR + 2 * NA:ABW].unsqueeze(1).broadcast_to([P, HS, RH])
                h4 = hs[k][:, :].rearrange("p (h c) -> p h c", c=C)
                d = dve.do(call(V.tensor_tensor, tmp[k][:, :].rearrange("p (s r) -> p s r", s=HS),
                                                   delta[k][:, :].rearrange("p (s r) -> p s r", s=HS), bs, ALU.mult),
                           d_delta)
                d = dve.do(call(V.tensor_tensor, tmp[k][:, :], tmp[k][:, :], out_t[:, :], ALU.mult), d, out_ready)
                d_skip = dve.do(call(V.tensor_tensor, h4[:, :, C - 1], h4[:, :, C - 1], tmp[k][:, :], ALU.add),
                                d, hs_ready)
                used[("tmp", k)] = d_skip
                yield
                g_hs = pool.do(call(G.tensor_tensor, h4[:, :, 0:C - 1], h4[:, :, 0:C - 1], Ah, ALU.mult),
                               a_A, hs_ready)
                used[("delta", k)] = g_hs
                d = dve.do(call(V.scalar_tensor_tensor,
                    out=Qs, in0=A2, scalar=1.0, in1=g[:, 2, :].unsqueeze(1).broadcast_to([P, HS, NA]),
                    op0=ALU.subtract, op1=ALU.mult), a_A, d_gain, used.get("Q"))
                used[("gate", k)] = d
                d = dve.do(call(V.tensor_tensor, Qh, Qh, out_t[:, :].unsqueeze(2).broadcast_to([P, H, C - 1]),
                                                   ALU.mult), d)
                d_hs = dve.do(call(V.tensor_tensor, h4[:, :, 0:C - 1], h4[:, :, 0:C - 1], Qh, ALU.add),
                              d, g_hs, d_skip)
                used["Q"] = used[("A", k)] = d_hs
                yield
                yield from tail(d_hs)

            hs_stored, y_ready, y_read = {}, {}, {}
            hs1_free, oT_read, tT_read = [], {}, {}
            att_read = []

            def attention_write(i):
                l = flow("m_hs0").dma(sp, hs[0][:, :], x[i], *hs1_free)
                lo_ = flow("m_oT").dma(sp, oTt[:, :, :], oT_d[i], oT_read.get(i - 1))
                a_hs = act.do(call(S.activation, hs[0][:, :], hs[0][:, :], ACT.Identity,
                                                   bias=nmr1[:, i:i + 1], scale=rstd1[:, i:i + 1]), l)
                for c0, cn, bank in ((0, H, 4), (H, ABW, 5)):
                    for kc in range(HCH):
                        mk = call(nc.tensor.matmul,
                            ps[:, bank, 0:cn], oTt[:, kc, :], wod1[:, kc, c0:c0 + cn],
                            start=(kc == 0), stop=(kc == HCH - 1))
                        if bank == 5 and kc == HCH - 1:
                            t = pe.do(mk)
                        else:
                            pe.quiet(mk, lo_, t_c, *(pair_read[0] or ()))
                oT_read[i] = t
                a_out = act.do(call(S.activation, outs1[:, :], ps[:, 4, :], ACT.Copy), t, *att_read)
                d_ab = dve.do(call(V.tensor_tensor, ab1[:, :], ps[:, 5, 0:ABW], gates_b[0][:, :], ALU.add),
                              t, t_c, *t_z, *att_read)
                pair_read[0] = (a_out, d_ab)
                yield

                def tail(d_hs):
                    att_read[:] = [d_hs]
                    hs_stored[i] = flow("m_hs_store").dma(sp, hs_d[i], hs[0][:, :], d_hs)
                    q2 = RD2 * HPC
                    turned = []
                    for q in range(4):
                        bank, free = one.take()
                        for j in range(4):
                            mk = call(nc.tensor.transpose,
                                ps[:, bank, P * j:P * j + P], hs[0][:, P * (4 * q + j):P * (4 * q + j) + P],
                                ident[:, :])
                            if j < 3:
                                pe.quiet(mk, d_hs, free)
                            else:
                                t = pe.do(mk)
                        on_act = q % 2 == 1
                        fn = (call(S.activation,
                            tT[q][:, :, :].rearrange("p a b -> p (a b)"), ps[:, bank, :], ACT.Copy)) if on_act else (
                            call(V.tensor_copy,
                                tT[q][:, :, :].rearrange("p a b -> p (a b)"), ps[:, bank, :]))
                        r = (act if on_act else dve).do(fn, t, tT_read.get(q))
                        one.read[bank] = r
                        turned.append(r)
                        if q % 2:
                            yield
                    hs1_free[:] = [t, hs_stored[i]]
                    for q in range(4):
                        for j in range(4):
                            jj = 4 * q + j
                            n = q2 if jj % 8 == 7 else q2 + 32
                            mk = call(nc.tensor.matmul,
                                ps[:, 4 + jj // 8, q2 * (jj % 8):q2 * (jj % 8) + n], tT[q][:, j, :],
                                read2[:, jj:jj + 2, :, :].rearrange("p a b c -> p (a b c)")[:, 0:n],
                                start=True, stop=True)
                            if j < 3:
                                pe.quiet(mk, turned[q], t_read2, z0, *(pair_read[0] or ()))
                            else:
                                t = pe.do(mk)
                        tT_read[q] = t
                    yield
                    yv = ps[:, 4:6, :].rearrange("p a (j o h) -> p a j o h", o=RD2, h=HPC)
                    for o in range(RD2):
                        for a_ in range(2):
                            d = dve.do(call(V.bn_stats, st[:, o, a_, :], yv[:, a_, :, o, :]), t)
                    for o in range(RD2):
                        d2 = dve.do(call(V.bn_aggr, my[:, o, :], st[:, o, :, :]), d)
                    d = dve.do(call(V.tensor_scalar, sc[:, 0, :], my[:, :, 1], EPS, None, ALU.add), d2,
                               used.get("sc"))
                    g = power_mhalf(sc[:, 1, :], sc[:, 0, :], d)
                    d = dve.do(call(V.scalar_tensor_tensor,
                        out=sc[:, 2, :], in0=my[:, :, 0], scalar=-1.0, in1=sc[:, 1, :],
                        op0=ALU.mult, op1=ALU.mult), g)
                    y = y2[i % TB]
                    for o in range(RD2):
                        for a_ in range(2):
                            a = act.do(call(S.activation,
                                y[:, o, 256 * a_:256 * a_ + 256].rearrange("p (j h) -> p j h", h=HPC),
                                yv[:, a_, :, o, :], ACT.Identity, bias=sc[:, 2, o:o + 1], scale=sc[:, 1, o:o + 1]),
                                d, y_read.get(i - TB))
                    used["sc"] = a
                    pair_read[0] = (a,)
                    y_ready[i] = a
                    yield
                yield from write(0, outs1, ab1, a_out, d_ab, a_hs, tail)

            hs2_free, slot_read, mlp_out = [], {}, {}

            def mlp_write(i):
                l = flow("m_hs1").dma(sp, hs[1][:, :], hs_d[i], hs_stored[i], *hs2_free)
                lx = flow("m_x").dma(sp, xt[:, :], x[i], used.get("x"))
                yield

                def tail(d_hs):
                    slot_read[i] = d_hs
                    g = pool.do(call(G.tensor_tensor, hs[1][:, :], hs[1][:, :], xt[:, :], ALU.add), d_hs, lx)
                    used["x"] = g
                    hs2_free[:] = [flow("m_x2_store").dma(sp, x2_d[i], hs[1][:, :], g)]
                    yield
                a_out, d_ab = mlp_out[i]
                yield from write(1, outs2[i % TB], ab2[i % TB], a_out, d_ab, l, tail)

            yT_ready, yT_free, yraw_read = {}, [None], {}

            def turn(blk):
                for k in range(RD2 * HCH):
                    o, hc = divmod(k, HCH)
                    bank, free = one.take()
                    for q in range(TB):
                        i = blk * TB + q
                        mk = call(nc.tensor.transpose,
                            ps[:, bank, P * q:P * q + P], y2[q][:, o, P * hc:P * hc + P], ident[:, :])
                        if q < TB - 1:
                            pe.quiet(mk, y_ready[i], free)
                        else:
                            t = pe.do(mk, y_ready[i])
                    s = k % 2
                    d = dve.do(call(V.tensor_scalar,
                        yraw[s][:, :], ps[:, bank, :], gam[:, k:k + 1], bet[:, k:k + 1], ALU.mult, ALU.add),
                        t, yraw_read.get(s), t_read2, t_c)
                    one.read[bank] = d
                    a = act.do(call(S.activation, yhi[:, k, :], yraw[s][:, :], ACT.Copy), d, yT_free[0])
                    g = pool.do(call(G.tensor_tensor,
                        ylo[:, k, :], yraw[s][:, :], yhi[:, k, :].bitcast(F32), ALU.subtract), a)
                    yraw_read[s] = g
                    yT_ready[(blk, k)] = g
                for q in range(TB):
                    y_read[blk * TB + q] = t

            win_read, win_loaded, win_turn = {}, {}, [0]
            w2_read, w2_loaded, w2_turn = {}, {}, [0]
            units = [(g2, mc) for _ in range(NBLK) for m2 in range(0, MCH, 2) for g2 in range(2)
                     for mc in (m2, m2 + 1)]

            def load_win(n):
                if n < len(units):
                    g2, mc = units[n]
                    s = n % WR
                    win_loaded[n] = flow(f"m_win{s}").dma(
                        sp, win[s][:, :, :, :].rearrange("p a c m -> p a (c m)"), win_d[2 * mc + g2],
                        win_read.get(n - WR))

            def load_w2(n):
                if n < NBLK * (TB // 2) * MCH:
                    s = n % W2R
                    w2_loaded[n] = flow(f"m_w2_{s}").dma(sp, w2[s][:, :], wod2T[n % MCH], w2_read.get(n - W2R))

            for n in range(WR):
                load_win(n)
            for n in range(W2R):
                load_w2(n)
            silu_read, hT_free = {}, [None]

            def mlp(blk):
                hready = {}
                for m2 in range(0, MCH, 2):
                    got = {}
                    for g2 in range(2):
                        for mc in (m2, m2 + 1):
                            n = win_turn[0]
                            win_turn[0] += 1
                            s = n % WR
                            bank, free = mlp_banks.take()
                            for ic in range(HCH):
                                k = g2 * HCH + ic
                                for p3, (wl, y) in enumerate(((0, yhi), (0, ylo), (1, yhi))):
                                    mk = call(nc.tensor.matmul,
                                        ps[:, bank, :], win[s][:, wl, ic, :], y[:, k, :],
                                        start=(ic == 0 and p3 == 0), stop=(ic == HCH - 1 and p3 == 2))
                                    ws = (win_loaded[n], yT_ready[(blk, k)], free)
                                    if ic == HCH - 1 and p3 == 2:
                                        t = pe.do(mk, *ws)
                                    else:
                                        pe.quiet(mk, *ws)
                            win_read[n] = t
                            load_win(n + WR)
                            got[(g2, mc)] = (bank, t)
                            if g2 == 1:
                                s2 = mc % 2
                                d = dve.do(call(V.tensor_tensor,
                                    hT[:, mc, :], silu[s2][:, :], ps[:, bank, :], ALU.mult), t, a2[mc], hT_free[0])
                                silu_read[s2] = d
                                mlp_banks.read[bank] = d
                                hready[mc] = d
                            elif mc % 2:
                                a2 = {}
                                for m in (m2, m2 + 1):
                                    gb, tg = got[(0, m)]
                                    s2 = m % 2
                                    a2[m] = act.do(call(S.activation,
                                        silu[s2][:, :], ps[:, gb, :], ACT.Silu), tg, silu_read.get(s2))
                                    mlp_banks.read[gb] = a2[m]
                                act.queue.append(call(S.preload_act_table_set, "natural_log_exp_and_others"))
                            yield
                yT_free[0] = t
                for q2 in range(TB // 2):
                    frees = [mlp_banks.read[k] for k in range(4)]
                    for k in range(MCH):
                        n = w2_turn[0]
                        w2_turn[0] += 1
                        s = n % W2R
                        for e in range(2):
                            q = 2 * q2 + e
                            for c0, cn, bank in ((0, H, 2 * e), (H, ABW, 2 * e + 1)):
                                mk = call(nc.tensor.matmul,
                                    ps[:, bank, 0:cn], hT[:, k, P * q:P * q + P], w2[s][:, c0:c0 + cn],
                                    start=(k == 0), stop=(k == MCH - 1))
                                ws = (hready[k], w2_loaded[n], *frees)
                                if bank == 3 or k == MCH - 1 and bank == 1:
                                    t = pe.do(mk, *ws)
                                else:
                                    pe.quiet(mk, *ws)
                            if k == MCH - 1:
                                i, r = blk * TB + q, slot_read.get((blk - 1) * TB + q)
                                assert blk == 0 or r is not None
                                a_out = act.do(call(S.activation,
                                    outs2[q][:, :], ps[:, 2 * e, :], ACT.Copy), t, r)
                                d_ab = dve.do(call(V.tensor_tensor,
                                    ab2[q][:, :], ps[:, 2 * e + 1, 0:ABW], gates_b[1][:, :], ALU.add), t, r)
                                mlp_banks.read[2 * e], mlp_banks.read[2 * e + 1] = a_out, d_ab
                                mlp_out[i] = (a_out, d_ab)
                        w2_read[n] = t
                        load_w2(n + W2R)
                        if k % 4 == 3:
                            yield
                hT_free[0] = t

            def attention_writes(blk):
                for i in range(blk * TB, blk * TB + TB):
                    yield from attention_write(i)

            def mlp_writes(blk):
                for i in range(blk * TB, blk * TB + TB):
                    yield from mlp_write(i)

            weave((attention_writes(0), 1))
            turn(0)
            for blk in range(NBLK):
                side = []
                if blk + 1 < NBLK:
                    side.append((attention_writes(blk + 1), 1))
                if blk:
                    side.append((mlp_writes(blk - 1), 1))
                weave((mlp(blk), 1), *side)
                if blk + 1 < NBLK:
                    turn(blk + 1)
            weave((mlp_writes(NBLK - 1), 1))

        def experts():
            place[0] = keep
            SCALE = 2.0 * NE
            wA = sb("e_A", [P, DCH, EW + NE])
            wB = sb("e_B", [P, D])
            brb = sb("e_br", [P, NE])
            ones = sb("e_ones", [P, P])
            asum = sb("e_Asum", [P, EW + NE])
            XR = 6
            xt = [sb(f"e_x{k}", [P, D]) for k in range(XR)]
            xT_ = [sb(f"e_xT{k}", [P, DCH, P]) for k in range(2)]
            st = [sb(f"e_stats{k}", [P, 4, 6]) for k in range(2)]
            mv = [sb(f"e_moments{k}", [P, 8]) for k in range(4)]
            low = [sb(f"e_low{k}", [P, EW + NE]) for k in range(2)]
            lw = [sb(f"e_weighted{k}", [P, EW]) for k in range(2)]
            rt = [sb(f"e_router{k}", [P, 3, NE]) for k in range(2)]
            lT = [sb(f"e_lowT{k}", [P, P]) for k in range(2)]
            V, S, G = nc.vector, nc.scalar, nc.gpsimd
            f = flow("e_const")
            f.dma(sp, wA[:, :, :], expA)
            f.dma(sp, wB[:, :], expB)
            t_c = f.dma(sp, brb[:, :], br.unsqueeze(0).broadcast_to([P, NE]))
            c1 = pool.do(call(G.memset, ones[:, :], 1.0))
            turned, lowb, outb = Banks([0, 1, 2, 3]), Banks([4, 5]), Banks([6, 7])
            bank, _ = lowb.take()
            for j in range(DCH):
                t = pe.do(call(nc.tensor.matmul, ps[:, bank, 0:EW + NE], ones[:, :], wA[:, j, :],
                                                       start=(j == 0), stop=(j == DCH - 1)), t_c, c1)
            t_asum = dve.do(call(V.tensor_copy, asum[:, :], ps[:, bank, 0:EW + NE]), t)
            lowb.read[bank] = t_asum
            x_free, loaded, norm, xT_ready, xT_read = {}, {}, {}, {}, {}
            low_read, lw_ready, lw_read, lT_ready, lT_read = {}, {}, {}, {}, {}

            def load(i):
                if i < NT:
                    loaded[i] = flow(f"e_x{i % XR}").dma(sp, xt[i % XR][:, :], x2_d[i], x_free.get(i - XR))

            def stage_norm(i):
                s = i % 2
                X = xt[i % XR]
                for q in range(4):
                    d = dve.do(call(V.bn_stats, st[s][:, q, :], X[:, 512 * q:512 * q + 512]), loaded[i])
                m = mv[i % 4]
                d = dve.do(call(V.bn_aggr, m[:, 0:2], st[s][:, :, :]), d)
                d1 = dve.do(call(V.tensor_scalar, m[:, 2:3], m[:, 0:1], -1.0, None, ALU.mult), d)
                d = dve.do(call(V.tensor_scalar, m[:, 3:4], m[:, 1:2], EPS, None, ALU.add), d)
                norm[i] = (d1, power_mhalf(m[:, 4:5], m[:, 3:4], d))
                ready = []
                for q in range(4):
                    bank, free = turned.take()
                    for j in range(4):
                        mk = call(nc.tensor.transpose,
                            ps[:, bank, P * j:P * j + P], X[:, P * (4 * q + j):P * (4 * q + j) + P], ident[:, :])
                        t = (pe.do if j == 3 else pe.quiet)(mk, loaded[i], free)
                    dst = xT_[s][:, 4 * q:4 * q + 4, :].rearrange("p a b -> p (a b)")
                    if q != 0:
                        r = act.do(call(S.activation, dst, ps[:, bank, :], ACT.Copy),
                                   t, xT_read.get(i - 2))
                    else:
                        r = dve.do(call(V.tensor_copy, dst, ps[:, bank, :]), t, xT_read.get(i - 2))
                    turned.read[bank] = r
                    ready.append(r)
                xT_ready[i] = ready

            def stage_low(i):
                s = i % 2
                m = mv[i % 4]
                bank, free = lowb.take()
                for j in range(DCH):
                    mk = call(nc.tensor.matmul, ps[:, bank, 0:EW + NE], xT_[s][:, j, :], wA[:, j, :],
                                                      start=(j == 0), stop=(j == DCH - 1))
                    t = (pe.do if j == DCH - 1 else pe.quiet)(mk, xT_ready[i][j // 4], free)
                xT_read[i] = t
                n1, n2 = norm[i]
                d = dve.do(call(V.scalar_tensor_tensor,
                    out=low[s][:, :], in0=asum[:, :], scalar=m[:, 2:3], in1=ps[:, bank, 0:EW + NE],
                    op0=ALU.mult, op1=ALU.add), t, n1, t_asum)
                lowb.read[bank] = d
                r = rt[s]
                d = dve.do(call(V.scalar_tensor_tensor,
                    out=r[:, 0, :], in0=low[s][:, EW:EW + NE], scalar=m[:, 4:5], in1=brb[:, :],
                    op0=ALU.mult, op1=ALU.add), d, n2)
                d = dve.do(call(V.tensor_reduce, m[:, 5:6], r[:, 0, :], AX_X, ALU.max, negate=True), d)
                a = act.do(call(S.activation, r[:, 1, :], r[:, 0, :], ACT.Exp, bias=m[:, 5:6],
                                                accum_out=m[:, 6:7]), d)
                d = dve.do(call(V.reciprocal, m[:, 7:8], m[:, 6:7]), a)
                d = dve.do(call(V.tensor_scalar, r[:, 2, :], r[:, 1, :], m[:, 7:8], SCALE, ALU.mult, ALU.mult), d)
                lw_ready[i] = dve.do(call(V.scalar_tensor_tensor,
                    out=lw[s][:, :].rearrange("p (e r) -> p e r", e=NE),
                    in0=low[s][:, 0:EW].rearrange("p (e r) -> p e r", e=NE), scalar=m[:, 4:5],
                    in1=r[:, 2, :].unsqueeze(2).broadcast_to([P, NE, RANK]), op0=ALU.mult, op1=ALU.mult),
                    d, lw_read.get(i - 2))

            def stage_turn(i):
                s = i % 2
                bank, free = lowb.take()
                t = pe.do(call(nc.tensor.transpose, ps[:, bank, 0:P], lw[s][:, :], ident[:, :]), lw_ready[i], free)
                lw_read[i] = t
                lT_ready[i] = act.do(call(S.activation, lT[s][:, :], ps[:, bank, 0:P], ACT.Copy),
                                     t, lT_read.get(i - 2))
                lowb.read[bank] = lT_ready[i]

            def stage_out(i):
                s = i % 2
                X = xt[i % XR]
                for q in range(4):
                    bank, free = outb.take()
                    t = pe.do(call(nc.tensor.matmul,
                        ps[:, bank, :], lT[s][:, :], wB[:, 512 * q:512 * q + 512], start=True, stop=True),
                        lT_ready[i], free)
                    d = dve.do(call(V.tensor_tensor,
                        X[:, 512 * q:512 * q + 512], ps[:, bank, :], X[:, 512 * q:512 * q + 512], ALU.add), t)
                    outb.read[bank] = d
                lT_read[i] = t
                x_free[i] = flow(f"e_out{i % XR}").dma(sp, out[i], X[:, :], d)

            for i in range(XR - 3):
                load(i)
            for n in range(NT + 3):
                if n < NT:
                    stage_norm(n)
                if 0 <= n - 2 < NT:
                    stage_turn(n - 2)
                if 0 <= n - 1 < NT:
                    stage_low(n - 1)
                if 0 <= n - 3 < NT:
                    stage_out(n - 3)
                load(n + XR - 3)

        project(0)
        barrier()
        attend(0, split_mlp_in)
        barrier()
        project(1)
        barrier()
        attend(1, None)
        barrier()
        mix()
        barrier()
        experts()
        sp.wait(*[f.last() for f in flows.values()])

        block = ctx.enter_context(nc.Block())

        def run(lane):
            for make in lane.queue:
                make()

        @block.tensor
        def _(e):
            run(pe)

        @block.scalar
        def _(e):
            run(act)

        @block.vector
        def _(e):
            run(dve)

        @block.gpsimd
        def _(e):
            run(pool)

        @block.sync
        def _(e):
            run(sp)


def kernel(x, pos_BxS, ctx_1024, L0_xattn_attn_read_w, L0_xattn_attn_read_g, L0_xattn_attn_read_b,
           L0_xattn_qkv_w, L0_xattn_attn_wod_w, L0_xattn_attn_wab_w, L0_xattn_attn_wab_b,
           L0_xattn_attn_du_w, L0_xattn_attn_du_b, L0_xattn_mlp_read_w, L0_xattn_mlp_read_g,
           L0_xattn_mlp_read_b, L0_xattn_mlp_wod_w, L0_xattn_mlp_wab_w, L0_xattn_mlp_wab_b,
           L0_xattn_mlp_du_w, L0_xattn_mlp_du_b, L0_ffn_A, L0_ffn_B, L0_ffn_Wr, L0_ffn_br):
    import concourse.bacc as bacc
    from concourse.bass_utils import run_bass_kernel_spmd

    def lay(a):
        return np.ascontiguousarray(a)

    def cols(w, n):
        return lay(np.transpose(np.reshape(w, (w.shape[0], n, P)), (2, 1, 0)))

    order = np.arange(H).reshape(NH, 2, HALF).transpose(1, 0, 2).reshape(-1)
    wqkv = np.asarray(L0_xattn_qkv_w)
    qkv = np.concatenate([cols(wqkv[0][order], HCH), cols(wqkv[1][order], HCH), cols(wqkv[2], HCH)], axis=1)

    def read_rep(w, outs):
        return lay(np.transpose(np.reshape(w, (DCH, HPC, outs, C)), (1, 3, 0, 2)).reshape(P, DCH * outs))

    xs = np.reshape(x, (NT, P, D))
    ctx = np.reshape(ctx_1024, (2, MCH, P, HCH, P))
    freq = (1.0 / 10000.0 ** (np.arange(HALF, dtype=np.float64) / HALF)).astype(np.float32)
    arrays = {
        "x": lay(xs),
        "xT": lay(np.transpose(np.reshape(x, (NT, P, DCH, P)), (0, 3, 2, 1))),
        "pos": lay(np.reshape(pos_BxS, (T,))),
        "inv_freq": lay(np.tile(freq, P // HALF).reshape(P, 1)),
        "ident": np.eye(P, dtype=np.float32),
        "causal": lay(np.where(np.arange(P)[None, :] > np.arange(P)[:, None], np.float32(NEG), np.float32(0))),
        "spread": lay((np.arange(P)[:, None] // C == np.arange(HPC)[None, :]).astype(np.float32)),
        "read1": read_rep(L0_xattn_attn_read_w, RD1),
        "gamma1": lay(np.reshape(L0_xattn_attn_read_g, (RD1 * HCH, P)).T),
        "beta1": lay(np.reshape(L0_xattn_attn_read_b, (RD1 * HCH, P)).T),
        "qkvT": lay(qkv),
        "wod1T": cols(np.concatenate([L0_xattn_attn_wod_w, L0_xattn_attn_wab_w], axis=0), HCH),
        "wab1_b": lay(L0_xattn_attn_wab_b),
        "du1T": lay(np.transpose(L0_xattn_attn_du_w)),
        "du1_b": lay(L0_xattn_attn_du_b),
        "read2": read_rep(L0_xattn_mlp_read_w, RD2),
        "gamma2": lay(np.reshape(L0_xattn_mlp_read_g, (RD2 * HCH, P)).T),
        "beta2": lay(np.reshape(L0_xattn_mlp_read_b, (RD2 * HCH, P)).T),
        "mlp_inT": lay(np.transpose(ctx, (1, 0, 4, 3, 2)).reshape(2 * MCH, P, HCH * P)),
        "wod2T": lay(np.transpose(np.concatenate([L0_xattn_mlp_wod_w, L0_xattn_mlp_wab_w], axis=0)).reshape(
            MCH, P, WOD)),
        "wab2_b": lay(L0_xattn_mlp_wab_b),
        "du2T": lay(np.transpose(L0_xattn_mlp_du_w)),
        "du2_b": lay(L0_xattn_mlp_du_b),
        "expA": cols(np.concatenate([np.reshape(L0_ffn_A, (EW, D)), L0_ffn_Wr], axis=0), DCH),
        "expB": lay(np.transpose(L0_ffn_B, (0, 2, 1)).reshape(EW, D)),
        "br": lay(L0_ffn_br),
    }
    nc = bacc.Bacc("TRN2", target_bir_lowering=False, num_devices=1)
    named, args = {}, []
    for name, a in arrays.items():
        named[f"in_{name}"] = a
        args.append(nc.dram_tensor(f"in_{name}", a.shape, mybir.dt.from_np(a.dtype), kind="ExternalInput").ap())
    out = nc.dram_tensor("out_x", [NT, P, D], F32, kind="ExternalOutput").ap()
    program(nc, *args, out)
    got = run_bass_kernel_spmd(nc, [named], core_ids=[0])
    return got.results[0]["out_x"].reshape(B, L, D)
```

```python
from contextlib import ExitStack

import numpy as np

import concourse.bass as bass
from concourse import mybir

F32 = mybir.dt.float32
F32R = mybir.dt.float32r
BF16 = mybir.dt.bfloat16
I32 = mybir.dt.int32
ALU = mybir.AluOpType
ACT = mybir.ActivationFunctionType
AX_X = mybir.AxisListType.X

P = 128
B, L, D = 2, 1024, 2048
H, C = 512, 4
NH = 16
HD = H // NH
HALF = HD // 2
RH = 16
HS = H // RH
DR = 8
M = 2048
NE, RANK = 8, 16
EPS = 1e-5
SSM_EPS = 1e-5
T = B * L
NT = T // P
TPB = L // P
BLK = 512
TB = BLK // P
NBLK = T // BLK
DCH = D // P
HCH = H // P
MCH = M // P
NA = (C - 1) * RH
GATES = 2 * NA + RH
ABW = DR + GATES
WOD = H + ABW
RD1, RD2 = 3, 2
HPC = P // C
EW = NE * RANK
NEG = -1e30


def call(op, *args, **options):
    return lambda: op(*args, **options)


class Lane:

    def __init__(self, name, engine, sem):
        self.name, self.e, self.sem, self.count, self.queue, self.seen = name, engine, sem, 0, [], {}

    def wait(self, *tickets):
        for t in tickets:
            if t is None:
                continue
            sem, value = t
            if self.seen.get(sem.name, 0) < value:
                self.seen[sem.name] = value
                self.queue.append(lambda e=self.e, s=sem, v=value: e.wait_ge(s, v))

    def do(self, make, *tickets):
        self.wait(*tickets)
        self.count += 1
        self.queue.append(lambda: make().then_inc(self.sem, 1))
        return (self.sem, self.count)

    def quiet(self, make, *tickets):
        self.wait(*tickets)
        self.queue.append(make)

    def last(self):
        return (self.sem, self.count) if self.count else None


class Flow:

    def __init__(self, sem):
        self.sem, self.count = sem, 0

    def dma(self, lane, dst, src, *tickets):
        lane.wait(*tickets)
        self.count += 16
        dst, src = (a.bitcast(F32) if a.dtype == F32R else a for a in (dst, src))
        lane.queue.append(lambda: lane.e.dma_start(dst, src).then_inc(self.sem, 16))
        return (self.sem, self.count)

    def last(self):
        return (self.sem, self.count) if self.count else None


class Banks:

    def __init__(self, banks):
        self.banks, self.turn, self.read = banks, 0, {b: None for b in banks}

    def take(self):
        b = self.banks[self.turn % len(self.banks)]
        self.turn += 1
        return b, self.read[b]


def weave(main, *sides):
    now, pool_free, live = 0.0, 0.0, [[g, 0.0] for g in sides]
    while main is not None or live:
        due = [item for item in live if item[1] <= now]
        if due:
            item = min(due, key=lambda item: item[1])
            step = next(item[0], "end")
            if step == "end":
                live.remove(item)
            else:
                on_pe, on_pool, wait = step
                now += on_pe
                if on_pool:
                    pool_free = max(now, pool_free) + on_pool
                item[1] = (pool_free if on_pool else now) + wait
        elif main is not None:
            step = next(main, "end")
            if step == "end":
                main = None
            else:
                now += step
        else:
            now = min(item[1] for item in live)


def program(nc, x, xT, pos, inv_freq, ident_in, causal_in, spread_in,
            read1_in, gamma1_in, beta1_in, qkvT, wod1T, wab1_b, du1T, du1_b,
            read2_in, gamma2_in, beta2_in, mlp_inT, wod2T, wab2_b, du2T, du2_b,
            expA, expB, br, out):
    with ExitStack() as ctx:
        sems = {}

        def sem(name):
            sems[name] = ctx.enter_context(nc.semaphore(name))
            return sems[name]

        pe = Lane("pe", nc.tensor, sem("pe_done"))
        act = Lane("act", nc.scalar, sem("act_done"))
        dve = Lane("dve", nc.vector, sem("dve_done"))
        pool = Lane("pool", nc.gpsimd, sem("pool_done"))
        sp = Lane("sp", nc.sync, None)
        flows = {}

        def flow(name):
            if name not in flows:
                flows[name] = Flow(sem("dma_" + name))
            return flows[name]

        ps = ctx.enter_context(nc.psum_tensor("ps", [P, 8, 512], F32))

        def dram(name, shape, dt=F32):
            return nc.dram_tensor(name, shape, dt, kind="Internal").ap()

        rope_d = dram("rope_tables", [2, HALF, T])
        qk_d = dram("qk_split", [B, 2, NH, 2, 2, HALF, L])
        oT_d = dram("attention_out", [NT, P, HCH, P])
        win_d = dram("mlp_in_split", [2 * MCH, P, 2, HCH * P])
        hs_d = dram("hidden_after_attention", [NT, P, D])
        x2_d = dram("x_after_layer", [NT, P, D])
        v_d = dram("values", [B, P, TPB, H])

        base = (nc.sbuf_base + 31) // 32 * 32
        top = nc.sbuf_usable_end
        place = [base]

        def sb(name, shape, dt=F32):
            size = int(np.prod(shape[1:])) * (2 if dt == BF16 else 4)
            size = (size + 31) // 32 * 32
            assert place[0] + size <= top, (name, place[0] + size - top)
            t = nc.alloc_sbuf_tensor_at(name, shape, dt, offset=place[0])
            place[0] += size
            return t

        def barrier():
            done = [l.last() for l in (pe, act, dve, pool)] + [f.last() for f in flows.values()]
            for l in (pe, act, dve, pool, sp):
                l.wait(*done)

        ident = sb("ident", [P, P])
        identb = sb("identb", [P, P], BF16)
        causalb = sb("causalb", [P, P], BF16)
        mhalf = sb("mhalf", [P, 4])
        rstd1 = sb("rstd1", [P, NT])
        negm1 = sb("negm1", [P, NT])
        nmr1 = sb("nmr1", [P, NT])
        keep = place[0]
        plan_end = {}

        c_ident = flow("ident").dma(sp, ident[:, :], ident_in)
        c_mhalf = pool.do(call(nc.gpsimd.memset, mhalf[:, :], -0.5))
        act.queue.append(call(nc.scalar.preload_act_table_set, "natural_log_exp_and_others"))

        def power_mhalf(dst, src, *tickets):
            n = dst.shape[1]
            return pool.do(call(nc.gpsimd.tensor_tensor, dst, src, mhalf[:, 0:n], ALU.pow), c_mhalf, *tickets)

        def project():
            place[0] = keep
            tag = "p_"
            XR, XTR, ZR, YR = 2, 2, 2, 6
            xt = [sb(tag + f"x{i}", [P, D]) for i in range(XR)]
            xTt = [sb(tag + f"xT{i}", [P, DCH, P]) for i in range(XTR)]
            zt = [sb(tag + f"z{i}", [P, DCH, RD1, HPC]) for i in range(ZR)]
            yn = [sb(tag + f"y{i}", [P, RD1, H]) for i in range(YR)]
            plan_end["project_reads"] = place[0]
            wq = sb(tag + "wqkv", [P, 3 * HCH, H])
            readw = sb(tag + "read1", [P, DCH, RD1, HPC])
            wsum = sb(tag + "read1_sum", [P, DCH * RD1 * HPC])
            gam = sb(tag + "gamma1", [P, RD1 * HCH])
            bet = sb(tag + "beta1", [P, RD1 * HCH])
            tab = [sb(tag + f"cos_sin{i}", [P, 2, BLK]) for i in range(2)]
            yT = sb(tag + "yT", [P, RD1 * HCH, BLK])
            rt = sb(tag + "rope", [P, 2, 4, BLK])
            hi = sb(tag + "rope_hi", [P, 2, 2, BLK], F32R)
            lo = sb(tag + "rope_lo", [P, 2, 2, BLK], F32R)
            vt = [sb(tag + f"v{i}", [P, TB, H]) for i in range(2)]
            st = sb(tag + "stats", [P, 2, 4, 6])
            mv = sb(tag + "moments", [P, 2, 8])
            sy = sb(tag + "ystats", [P, 2, RD1, 6])
            my = sb(tag + "ymoments", [P, 2, RD1, 2])
            sc = sb(tag + "yscale", [P, 2, 4, RD1])

            f = flow("p_const")
            spread = sb(tag + "spread", [P, HPC])
            wrep = sb(tag + "read1_rep", [P, DCH * RD1])
            ones = sb(tag + "ones", [P, P])
            f.dma(sp, spread[:, :], spread_in)
            c_rep = f.dma(sp, wrep[:, :], read1_in)
            c_ones = pool.do(call(nc.gpsimd.memset, ones[:, :], 1.0))

            x_read, xT_read, z_read = {}, {}, {}

            def load(i):
                c = flow(f"xT{i % XTR}").dma(sp, xTt[i % XTR][:, :, :], xT[i], xT_read.get(i - XTR))
                a = flow(f"x{i % XR}").dma(sp, xt[i % XR][:, :], x[i], x_read.get(i - XR))
                return a, c

            loaded = {0: load(0), 1: load(1)}
            posi = sb(tag + "pos_i", [P, T // (P // HALF)], I32)
            invf = sb(tag + "inv_freq", [P, 1])
            cf = sb(tag + "causal_f32", [P, P])
            flow("rope_in").dma(sp, invf[:, :], inv_freq)
            for k in range(P // HALF):
                w8 = T // (P // HALF)
                t_pos = flow("rope_in").dma(sp, posi[HALF * k:HALF * k + HALF, :],
                                            pos[k * w8:(k + 1) * w8].unsqueeze(0).broadcast_to([HALF, w8]))
            c_causal = flow("causal").dma(sp, cf[:, :], causal_in)
            g = flow("p_scale")
            g.dma(sp, gam[:, :], gamma1_in)
            t_gb = g.dma(sp, bet[:, :], beta1_in)
            t_w = flow("wqkv").dma(sp, wq[:, :, :], qkvT)
            flat = readw[:, :, :, :].rearrange("p a b c -> p (a b) c")
            n48 = DCH * RD1
            t_read = dve.do(call(nc.vector.tensor_tensor,
                flat, wrep[:, :].unsqueeze(2).broadcast_to([P, n48, HPC]),
                spread[:, :].unsqueeze(1).broadcast_to([P, n48, HPC]), ALU.mult), c_rep)
            flat1 = readw[:, :, :, :].rearrange("p a b c -> p (a b c)")
            for n in range(3):
                t_sum = pe.do(call(nc.tensor.matmul, ps[:, n, :], ones[:, :], flat1[:, 512 * n:512 * n + 512],
                                                           start=True, stop=True), t_read, c_ones)
            t_wsum = dve.do(call(nc.vector.tensor_copy,
                wsum[:, :], ps[:, 0:3, :].rearrange("p a b -> p (a b)")), t_sum)

            dve.do(call(nc.vector.tensor_copy, identb[:, :], ident[:, :]), c_ident)
            dve.do(call(nc.vector.tensor_copy, causalb[:, :], cf[:, :]), c_causal)

            def rotary_tables():
                NB8 = P // HALF
                W8 = T // NB8
                ang = sb(tag + "angle", [P, W8])
                kk = sb(tag + "turns", [P, W8])
                sn = sb(tag + "sine", [P, 2, W8])
                TWO_PI = 2 * np.pi
                C1 = 6.28125
                C2 = float(np.float32(np.floor((TWO_PI - C1) * 2 ** 21) / 2 ** 21))
                C3 = float(np.float32(TWO_PI - C1 - C2))
                MAGIC = 1.5 * 2 ** 23
                V = nc.vector
                d = dve.do(call(V.tensor_copy, ang[:, :], posi[:, :]), t_pos)
                d = dve.do(call(V.tensor_scalar, ang[:, :], ang[:, :], invf[:, 0:1], None, ALU.mult), d)
                d = dve.do(call(V.tensor_scalar, kk[:, :], ang[:, :], 1.0 / TWO_PI, MAGIC, ALU.mult, ALU.add), d)
                d = dve.do(call(V.tensor_scalar, kk[:, :], kk[:, :], MAGIC, None, ALU.subtract), d)
                for cc in (C1, C2, C3):
                    d = dve.do(call(V.scalar_tensor_tensor,
                        out=ang[:, :], in0=kk[:, :], scalar=-cc, in1=ang[:, :], op0=ALU.mult, op1=ALU.add), d)
                PI = 3.1415925
                d = dve.do(call(V.tensor_scalar, sn[:, 0, :], ang[:, :], float(np.pi / 2), None, ALU.add), d)
                d = dve.do(call(V.tensor_scalar, kk[:, :], sn[:, 0, :], PI, -TWO_PI, ALU.is_gt, ALU.mult), d)
                d = dve.do(call(V.tensor_tensor, sn[:, 0, :], sn[:, 0, :], kk[:, :], ALU.add), d)
                d = dve.do(call(V.tensor_scalar, sn[:, 0, :], sn[:, 0, :], PI, -PI, ALU.min, ALU.max), d)
                d = dve.do(call(V.tensor_scalar, sn[:, 1, :], ang[:, :], PI, -PI, ALU.min, ALU.max), d)
                a = act.do(call(nc.scalar.activation, sn[:, :, :], sn[:, :, :], ACT.Sin), d)
                act.queue.append(call(nc.scalar.preload_act_table_set, "natural_log_exp_and_others"))
                for k in range(NB8):
                    for w in range(2):
                        t = flow("rope_out").dma(sp, rope_d[w, :, k * W8:(k + 1) * W8],
                                                 sn[HALF * k:HALF * k + HALF, w, :], a)
                return t

            tab_loaded, tab_read = {}, {}

            def load_tab(blk):
                s = blk % 2
                for k in range(P // HALF):
                    for w in range(2):
                        tab_loaded[blk] = flow(f"rope_tab{s}").dma(
                            sp, tab[s][HALF * k:HALF * k + HALF, w, :], rope_d[w, :, blk * BLK:(blk + 1) * BLK],
                            t_rope, tab_read.get(blk - 2))

            y_read = t_wsum
            y_ready, y_turned = {}, {}

            def read(i):
                nonlocal y_read
                n, s = i, i % 2
                lx, lxT = loaded.pop(i)
                V = nc.vector
                for q in range(4):
                    d = dve.do(call(V.bn_stats, st[:, s, q, :], xt[i % XR][:, 512 * q:512 * q + 512]), lx)
                x_read[i] = d
                d = dve.do(call(V.bn_aggr, mv[:, s, 0:2], st[:, s, :, :]), d)
                d = dve.do(call(V.tensor_scalar, negm1[:, n:n + 1], mv[:, s, 0:1], -1.0, None, ALU.mult), d)
                d = dve.do(call(V.tensor_scalar, mv[:, s, 2:3], mv[:, s, 1:2], EPS, None, ALU.add), d)
                g = power_mhalf(rstd1[:, n:n + 1], mv[:, s, 2:3], d)
                zw = RD1 * HPC
                for j in range(DCH):
                    mk = call(nc.tensor.matmul,
                        ps[:, j // 4, zw * (j % 4):zw * (j % 4) + zw], xTt[i % XTR][:, j, :],
                        readw[:, j, :, :].rearrange("p a b -> p (a b)"), start=True, stop=True)
                    if j < DCH - 1:
                        pe.quiet(mk, lxT, t_read, y_read)
                    else:
                        t = pe.do(mk)
                xT_read[i] = t
                if i + 2 < NT:
                    loaded[i + 2] = load(i + 2)
                yield 3.8, 0, 0.3
                z = zt[i % ZR]
                d = dve.do(call(V.scalar_tensor_tensor,
                    out=z[:, :, :, :].rearrange("p (k a) b c -> p k (a b c)", k=4),
                    in0=wsum[:, :].rearrange("p (k n) -> p k n", k=4),
                    scalar=negm1[:, n:n + 1], in1=ps[:, 0:4, 0:4 * zw], op0=ALU.mult, op1=ALU.add),
                    t, t_wsum, z_read.get(i - ZR), d)
                y_read = d
                for o in range(RD1):
                    e = dve.do(call(V.bn_stats, sy[:, s, o, :], z[:, :, o, :]), d)
                for o in range(RD1):
                    e2 = dve.do(call(V.bn_aggr, my[:, s, o, :], sy[:, s, o, :]), e)
                e = dve.do(call(V.tensor_tensor, mv[:, s, 3:4], rstd1[:, n:n + 1], rstd1[:, n:n + 1], ALU.mult), g)
                dve.do(call(V.tensor_tensor, nmr1[:, n:n + 1], rstd1[:, n:n + 1], negm1[:, n:n + 1], ALU.mult), g)
                e = dve.do(call(V.tensor_scalar, sc[:, s, 0, :], my[:, s, :, 1], mv[:, s, 3:4], EPS,
                                                   ALU.mult, ALU.add), e, e2)
                g = power_mhalf(sc[:, s, 1, :], sc[:, s, 0, :], e)
                e = dve.do(call(V.tensor_scalar, sc[:, s, 2, :], sc[:, s, 1, :], rstd1[:, n:n + 1], None,
                                                   ALU.mult), g)
                e = dve.do(call(V.scalar_tensor_tensor,
                    out=sc[:, s, 3, :], in0=my[:, s, :, 0], scalar=-1.0, in1=sc[:, s, 2, :],
                    op0=ALU.mult, op1=ALU.mult), e)
                for o in range(RD1):
                    a = act.do(call(nc.scalar.activation,
                        yn[i % YR][:, o, :].rearrange("p (a b) -> p a b", b=HPC), z[:, :, o, :], ACT.Identity,
                        bias=sc[:, s, 3, o:o + 1], scale=sc[:, s, 2, o:o + 1]), e, y_turned.get(i - YR))
                z_read[i] = y_ready[i] = a
                yield 0, 0, 1.5

            ring = Banks([4, 5, 6, 7])
            yT_read = [None]

            def reads(blk):
                for i in range(blk * TB, blk * TB + TB):
                    yield from read(i)

            def turn(blk):
                ready = []
                for k in range(RD1 * HCH):
                    o, hc = divmod(k, HCH)
                    bank, free = ring.take()
                    for q in range(TB):
                        i = blk * TB + q
                        mk = call(nc.tensor.transpose,
                            ps[:, bank, P * q:P * q + P], yn[i % YR][:, o, P * hc:P * hc + P], ident[:, :])
                        if q < TB - 1:
                            pe.quiet(mk, y_ready[i], free, c_ident)
                        else:
                            t = pe.do(mk, y_ready[i])
                    if k % 2:
                        r = dve.do(call(nc.vector.tensor_scalar,
                            yT[:, k, :], ps[:, bank, :], gam[:, k:k + 1], bet[:, k:k + 1], ALU.mult, ALU.add),
                            t, yT_read[0], t_gb)
                    else:
                        r = act.do(call(nc.scalar.activation,
                            yT[:, k, :], ps[:, bank, :], ACT.Identity, bias=bet[:, k:k + 1],
                            scale=gam[:, k:k + 1]), t, yT_read[0], t_gb)
                    ring.read[bank] = r
                    ready.append(r)
                    yield 0.5
                for q in range(TB):
                    y_turned[blk * TB + q] = t
                yT_ready[blk] = ready

            yT_ready = {}
            split_stored = {0: None, 1: None}
            qk_stored = []

            def qkv(blk):
                ready = yT_ready[blk]
                b, t0 = divmod(blk * BLK, L)
                for pair in range(4):
                    w, oc = divmod(pair, 2)
                    s = pair % 2
                    got = []
                    for half in range(2):
                        bank, free = ring.take()
                        col = (half * 2 + oc) * P
                        for ic in range(HCH):
                            mk = call(nc.tensor.matmul,
                                ps[:, bank, :], wq[:, w * HCH + ic, col:col + P], yT[:, w * HCH + ic, :],
                                start=(ic == 0), stop=(ic == HCH - 1))
                            if ic < HCH - 1:
                                pe.quiet(mk, free, t_qs, ready[w * HCH + ic])
                            else:
                                t = pe.do(mk, ready[w * HCH + ic])
                        got.append((bank, t))
                        yield 3.5
                    V = nc.vector
                    cs, sn_ = tab[blk % 2][:, 0, :], tab[blk % 2][:, 1, :]
                    (b1, p1), (b2, p2) = got
                    dve.do(call(V.tensor_tensor, rt[:, s, 0, :], ps[:, b1, :], cs, ALU.mult), p1, tab_loaded[blk], rt_read[s])
                    r1 = dve.do(call(V.tensor_tensor, rt[:, s, 3, :], ps[:, b1, :], sn_, ALU.mult))
                    dve.do(call(V.tensor_tensor, rt[:, s, 1, :], ps[:, b2, :], sn_, ALU.mult), p2)
                    r2 = dve.do(call(V.tensor_tensor, rt[:, s, 2, :], ps[:, b2, :], cs, ALU.mult))
                    ring.read[b1], ring.read[b2] = r1, r2
                    tab_read[blk] = r2
                    G = nc.gpsimd
                    ga = pool.do(call(G.tensor_tensor, rt[:, s, 0, :], rt[:, s, 0, :], rt[:, s, 1, :],
                                                         ALU.subtract), r2)
                    gb = pool.do(call(G.tensor_tensor, rt[:, s, 2, :], rt[:, s, 2, :], rt[:, s, 3, :], ALU.add))
                    for h_, slot, gt in ((0, 0, ga), (1, 2, gb)):
                        ah = act.do(call(nc.scalar.activation,
                            hi[:, s, h_, :], rt[:, s, slot, :], ACT.Copy), gt, split_stored[s])
                        gl = pool.do(call(G.tensor_tensor,
                            lo[:, s, h_, :], rt[:, s, slot, :], hi[:, s, h_, :].bitcast(F32), ALU.subtract), ah)
                        for hl, buf, tt in ((0, hi, ah), (1, lo, gl)):
                            stt = flow(f"split{s}").dma(
                                sp, qk_d[b, w, 8 * oc:8 * oc + 8, hl, h_, :, t0:t0 + BLK], buf[:, s, h_, :], tt)
                    rt_read[s] = gl
                    split_stored[s] = stt
                for q in range(TB):
                    bank, free = ring.take()
                    for ic in range(HCH):
                        mk = call(nc.tensor.matmul,
                            ps[:, bank, :], yT[:, 2 * HCH + ic, P * q:P * q + P], wq[:, 2 * HCH + ic, :],
                            start=(ic == 0), stop=(ic == HCH - 1))
                        if ic < HCH - 1:
                            pe.quiet(mk, free, t_w, ready[2 * HCH + ic])
                        else:
                            t = pe.do(mk, ready[2 * HCH + ic])
                    ring.read[bank] = a = act.do(call(nc.scalar.activation,
                        vt[blk % 2][:, q, :], ps[:, bank, :], ACT.Copy), t, v_stored.get(blk - 2))
                    yield 3.5
                yT_read[0] = t

                k0 = t0 // P
                v_stored[blk] = flow(f"v_store{blk % 2}").dma(
                    sp, v_d[b, :, k0:k0 + TB, :], vt[blk % 2][:, :, :], a)
                if blk + 2 < NBLK:
                    load_tab(blk + 2)

            rt_read, v_stored = {0: None, 1: None}, {}
            weave(None, reads(0))
            t_qs = dve.do(call(nc.vector.tensor_scalar, wq[:, 0:HCH, :], wq[:, 0:HCH, :],
                                                          float(1.0 / np.float32(np.sqrt(HD))), None, ALU.mult), t_w)
            t_rope = rotary_tables()
            load_tab(0)
            load_tab(1)
            weave(turn(0))
            for blk in range(NBLK):
                if blk + 1 < NBLK:
                    weave(qkv(blk), reads(blk + 1))
                    weave(turn(blk + 1))
                else:
                    attention = attend(split_mlp_in, mix, y_turned[NT - 1], first_stored)
                    next(attention)
                    weave(qkv(blk))
                if blk == L // BLK - 1:
                    first_stored = [split_stored[0], split_stored[1], v_stored[0], v_stored[1]]
            barrier()
            for _ in attention:
                pass

        def attend(extra, following, reads_done, first_stored):
            tag = "a_"
            place[0] = keep
            NS = 8
            qs = [sb(tag + f"q{i}", [P, L], F32R) for i in range(NS)]
            ks = [sb(tag + f"k{i}", [P, L], F32R) for i in range(NS)]
            VR, PR, PTR = 3, 3, 3
            vt = [sb(tag + f"v{i}", [P, TPB, P]) for i in range(VR)]
            assert place[0] <= plan_end["project_reads"]
            head_loaded, head_read, v_loaded, v_read = {}, {}, {}, {}

            def load_head(n):
                b, h = divmod(n, NH)
                s = n % NS
                f = flow(f"head{s}")
                src_q = qk_d[b, 0, h].rearrange("a c r t -> (a c r) t")
                src_k = qk_d[b, 1, h].rearrange("a c r t -> a (c r) t")
                free = head_read.get(n - NS, reads_done)
                for r in range(2):
                    f.dma(sp, qs[s][64 * r:64 * r + 64, :], src_q, free)
                for r in range(4):
                    t = f.dma(sp, ks[s][32 * r:32 * r + 32, :], src_k[r // 2])
                head_loaded[n] = t

            def load_v(f4):
                b, h4 = divmod(f4, NH // 4)
                s = f4 % VR
                v_loaded[f4] = flow(f"v_load{s}").dma(
                    sp, vt[s][:, :, :], v_d[b, :, :, P * h4:P * h4 + P], v_read.get(f4 - VR, reads_done))

            fours = B * NH // 4
            sp.wait(*first_stored)
            load_head(0)
            load_head(1)
            load_v(0)
            load_head(2)
            load_head(3)
            yield
            pt = [sb(tag + f"p{i}", [P, L]) for i in range(PR)]
            pT = [sb(tag + f"pT{i}", [P, TPB, BLK]) for i in range(PTR)]
            negmax = sb(tag + "negmax", [P, 4, 2])
            rsum = sb(tag + "rowsum", [P, 2, 4 * TB])
            rinv = sb(tag + "rowinv", [P, 4 * TB])
            rb = sb(tag + "rowinv_wide", [P, 4 * TB, HD])
            rT = sb(tag + "rowinv_T", [P, BLK])
            oT = [sb(tag + f"oT{i}", [P, BLK]) for i in range(2)]
            aux = extra(tag)
            plan_end["attend"] = place[0]
            early = following()

            groups = [(f4, g) for f4 in range(fours) for g in range(2)]
            sets = [(gi, f4, g, heads) for gi, (f4, g) in enumerate(groups)
                    for heads in (((0, 1), (2, 3)) if g == 0 else ((0,), (1,), (2,), (3,)))]
            units = [(si, q) for si in range(len(sets)) for q in range(TB)]
            SB = [0, 2]
            turned = Banks([4, 5, 7])
            scores_read, max_done, exp_done, p_read = {}, {}, {}, {}
            pT_ready, pT_read = {}, {}
            load = {"act": 0.0, "dve": 0.0}

            def flat(bank):
                return ps[:, bank:bank + 2, :].rearrange("p a b -> p (a b)")

            def view(n, t):
                si, q = units[n]
                g, heads = sets[si][2:]
                klen = (g * TB + q + 1) * P
                return t.rearrange("p (a k) -> p a k", a=len(heads))[:, :, 0:klen], klen

            def scores(n):
                si, q = units[n]
                gi, f4, g, heads = sets[si]
                bank, qt, free = SB[n % 2], g * TB + q, scores_read.get(n - 2)
                klen = (qt + 1) * P
                for j, hh in enumerate(heads):
                    h = 4 * f4 + hh
                    s = h % NS
                    for k0 in range(0, klen, 512):
                        kn = min(512, klen - k0)
                        pe.quiet(call(nc.tensor.matmul,
                            ps[:, bank + j + k0 // 512, 0:kn], qs[s][:, qt * P:qt * P + P], ks[s][:, k0:k0 + kn],
                            start=True, stop=k0 + kn < klen), head_loaded[h], free)
                    t = pe.do(call(nc.tensor.matmul,
                        ps[:, bank + j + (klen - 1) // 512, (klen - P) % 512:(klen - P) % 512 + P],
                        identb[:, :], causalb[:, :], start=False, stop=True))
                    if g == 1 and q == TB - 1:
                        head_read[h] = t
                v, _ = view(n, flat(bank))
                max_done[n] = dve.do(call(nc.vector.tensor_reduce,
                    negmax[:, n % 4, 0:len(heads)], v, AX_X, ALU.max, negate=True), t, exp_done.get(n - 4))
                load["dve"] += klen * len(heads) / .96 + 80

            def exponentials(n):
                si, q = units[n]
                gi, f4, g, heads = sets[si]
                src, klen = view(n, flat(SB[n % 2]))
                dst, _ = view(n, pt[n % PR][:, :])
                for j, hh in enumerate(heads):
                    col = q * 4 + hh
                    a = act.do(call(nc.scalar.activation,
                        dst[:, j, :], src[:, j, :], ACT.Exp, bias=negmax[:, n % 4, j:j + 1],
                        accum_out=rsum[:, gi % 2, col:col + 1]), max_done[n], p_read.get(n - PR), sum_read.get(gi - 2))
                    load["act"] += klen / 1.2 + 280
                exp_done[n] = scores_read[n] = last_exp[gi] = a

            sum_read, last_exp = {}, {}

            def turn(n):
                si, q = units[n]
                gi, f4, g, heads = sets[si]
                nk = g * TB + q + 1
                src, _ = view(n, pt[n % PR][:, :])
                kept = pT[si % PTR][:, :, :].rearrange("p (a k) c -> p a k c", a=len(heads))
                blocks = [(j, k) for j in range(len(heads)) for k in range(nk)]
                parts = [blocks] if len(blocks) <= 4 else [
                    [(j, k) for k in range(k0, min(k0 + 4, nk))] for j in range(len(heads)) for k0 in range(0, nk, 4)]
                for part in parts:
                    bank, free = turned.take()
                    for m, (j, k) in enumerate(part):
                        mk = call(nc.tensor.transpose,
                            ps[:, bank, P * m:P * m + P], src[:, j, P * k:P * k + P], ident[:, :])
                        if m < len(part) - 1:
                            pe.quiet(mk, exp_done[n], free)
                        else:
                            t = pe.do(mk, exp_done[n], free)
                    (j0, k0), (j1, k1) = part[0], part[-1]
                    dst = kept[:, j0:j1 + 1, k0:k1 + 1, P * q:P * q + P]
                    got = ps[:, bank, 0:P * len(part)].rearrange("p (a k b) -> p a k b", a=j1 + 1 - j0, b=P)
                    free = pT_read.get(si - PTR)
                    if load["act"] < load["dve"]:
                        r = act.do(call(nc.scalar.activation, dst, got, ACT.Copy), t, free)
                        load["act"] += len(part) * P / 1.2 + 90
                        pT_ready.setdefault(si, {})["act"] = r
                    else:
                        r = dve.do(call(nc.vector.tensor_copy, dst, got), t, free)
                        load["dve"] += len(part) * P / .96 + 80
                        pT_ready.setdefault(si, {})["dve"] = r
                    turned.read[bank] = r
                p_read[n] = t

            o_read = {"o": None}
            oT_stored = {}

            def values(si):
                gi, f4, g, heads = sets[si]
                s = f4 % VR
                nk = (g + 1) * TB
                kept = pT[si % PTR][:, :, :].rearrange("p (a k) c -> p a k c", a=len(heads))
                w = list(pT_ready[si].values()) + [v_loaded[f4], o_read["o"]]
                ends = heads[-1] == 3
                if ends:
                    spread = spread_sums(gi)
                for j, hh in enumerate(heads):
                    for k in range(nk):
                        q0 = max(0, k * P - g * BLK)
                        mk = call(nc.tensor.matmul,
                            ps[32 * hh:32 * hh + 32, 6, q0:BLK], vt[s][:, k, HD * hh:HD * hh + HD],
                            kept[:, j, k, q0:BLK], start=(k == 0), stop=(k == nk - 1))
                        if k == nk - 1 and hh == heads[-1]:
                            t = pe.do(mk, *w)
                        else:
                            pe.quiet(mk, *w)
                            if (4 * j + k) % 3 == 2:
                                yield
                                if ends and j + k == 2:
                                    sums = turn_sums(spread)
                pT_read[si] = v_read[f4] = t
                if ends:
                    finish(gi, t, sums)

            def spread_sums(gi):
                d = dve.do(call(nc.vector.reciprocal, rinv[:, :], rsum[:, gi % 2, :]), last_exp[gi])
                sum_read[gi] = d
                return dve.do(call(nc.vector.tensor_copy,
                    rb[:, :, :], rinv[:, :].unsqueeze(2).broadcast_to([P, 4 * TB, HD])), d, o_read.get("rb"))

            def turn_sums(spread):
                bank, free = turned.take()
                for q in range(TB):
                    t = pe.do(call(nc.tensor.transpose,
                        ps[:, bank, P * q:P * q + P], rb[:, 4 * q:4 * q + 4, :].rearrange("p a b -> p (a b)"),
                        ident[:, :]), spread, free)
                o_read["rb"] = t
                turned.read[bank] = act.do(call(nc.scalar.activation, rT[:, :], ps[:, bank, :], ACT.Copy),
                                           t, o_read["o"])
                return turned.read[bank]

            def finish(gi, t_values, sums):
                f4, g = groups[gi]
                b, h4 = divmod(f4, NH // 4)
                s = gi % 2
                d = dve.do(call(nc.vector.tensor_tensor, oT[s][:, :], ps[:, 6, :], rT[:, :], ALU.mult),
                           t_values, sums, oT_stored.get(gi - 2))
                o_read["o"] = d
                i0 = b * TPB + g * TB
                for q in range(TB):
                    oT_stored[gi] = flow(f"oT{s}").dma(sp, oT_d[i0 + q, :, h4, :], oT[s][:, P * q:P * q + P], d)

            for n in range(2):
                scores(n)
                exponentials(n)
            product = iter(())
            for n in range(len(units)):
                si, q = units[n]
                gi, f4, g, heads = sets[si]
                if g == 0 and heads[0] == 0 and q == 2 and f4 + 1 < fours:
                    for h in range(4):
                        load_head(4 * (f4 + 1) + h)
                    load_v(f4 + 1)
                if n + 2 < len(units):
                    scores(n + 2)
                turn(n)
                if n + 2 < len(units):
                    exponentials(n + 2)
                if q == 0 and si:
                    for _ in product:
                        pass
                    product = values(si - 1)
                next(product, None)
                if n % 4 == 0:
                    next(aux, None)
                if n in (12, len(units) - 8):
                    next(early)
            for _ in aux:
                pass
            for _ in product:
                pass
            for _ in values(len(sets) - 1):
                pass
            barrier()
            for _ in early:
                pass

        def split_mlp_in(tag):
            raw = [sb(tag + f"w_raw{i}", [P, HCH * P]) for i in range(2)]
            two = [sb(tag + f"w_two{i}", [P, 2, HCH * P], F32R) for i in range(2)]

            def steps():
                done, stored, read_in = {}, {}, {}

                def load(u):
                    if u < 2 * MCH:
                        read_in[u] = flow(f"w_raw{u % 2}").dma(sp, raw[u % 2][:, :], mlp_inT[u], done.get(u - 2))

                load(0)
                for u in range(2 * MCH):
                    s = u % 2
                    load(u + 1)
                    l = read_in[u]
                    g = pool.do(call(nc.gpsimd.tensor_scalar,
                        two[s][:, 0, :], raw[s][:, :], 1.0, None, ALU.mult), l, stored.get(u - 2))
                    g = pool.do(call(nc.gpsimd.tensor_tensor,
                        two[s][:, 1, :], raw[s][:, :], two[s][:, 0, :].bitcast(F32), ALU.subtract), g)
                    done[u] = g
                    yield
                    stored[u] = flow(f"w_two{s}").dma(sp, win_d[u], two[s][:, :, :], g)
            return steps()

        def mix():
            gates_b, duT, dlT = [], [], []
            f = flow("m_const")
            place[0] = plan_end["attend"]
            WR, W2R = 4, 3
            wod1 = sb("m_wod1", [P, HCH, WOD])
            read2 = sb("m_read2", [P, DCH + 1, RD2, HPC])
            gam = sb("m_gamma2", [P, RD2 * HCH])
            bet = sb("m_beta2", [P, RD2 * HCH])
            wrep = sb("m_read2_rep", [P, DCH * RD2])
            spread = sb("m_spread", [P, HPC])
            oTt = sb("m_oT", [P, HCH, P])
            win = [sb(f"m_win{k}", [P, 2, HCH, P], F32R) for k in range(WR)]
            w2 = [sb(f"m_wod2_{k}", [P, WOD]) for k in range(W2R)]
            plan_end["mix_weights"] = place[0]
            for k in range(2):
                gates_b.append(sb(f"m_gate_bias{k}", [P, ABW]))
                duT.append(sb(f"m_duT{k}", [P, H]))
                dlT.append(sb(f"m_lowT{k}", [P, P]))
            place[0] = keep
            hs = [sb(f"m_hs{k}", [P, D]) for k in range(2)]
            xt = [None, sb("m_x", [P, D])]
            Ab = [sb(f"m_A{k}", [P, NA * HS]) for k in range(2)]
            outs2 = [sb(f"m_mlp_out{k}", [P, H]) for k in range(TB)]
            ab2 = [sb(f"m_mlp_ab{k}", [P, ABW]) for k in range(TB)]
            delta = [sb(f"m_delta{k}", [P, H]) for k in range(2)]
            tmp = [sb(f"m_tmp{k}", [P, H]) for k in range(2)]
            g1 = [sb(f"m_gate{k}", [P, 4, NA]) for k in range(2)]
            experts_place = place[0]
            y2 = [sb(f"m_y{k}", [P, RD2, H]) for k in range(TB)]
            yhi = sb("m_yhi", [P, RD2 * HCH, BLK], F32R)
            ylo = sb("m_ylo", [P, RD2 * HCH, BLK], F32R)
            first_loads_end = place[0]
            tT = sb("m_hsT", [P, 4, BLK])
            outs1 = sb("m_att_out", [P, H])
            ab1 = sb("m_att_ab", [P, ABW])
            st = sb("m_stats", [P, 2, RD2, 2, 6])
            my = sb("m_moments", [P, 2, RD2, 2])
            sc = sb("m_scale", [P, 2, 3, RD2])
            yraw = [sb(f"m_yraw{k}", [P, BLK]) for k in range(2)]
            silu = [sb(f"m_silu{k}", [P, BLK]) for k in range(2)]
            hT = sb("m_hT", [P, MCH, BLK])
            assert place[0] <= plan_end["attend"], place[0] - plan_end["attend"]

            t_wod1 = flow("m_wod1").dma(sp, wod1[:, :, :], wod1T)
            f.dma(sp, gam[:, :], gamma2_in)
            f.dma(sp, bet[:, :], beta2_in)
            flow("m_read2").dma(sp, spread[:, :], spread_in)
            t_rep = flow("m_read2").dma(sp, wrep[:, :], read2_in)
            t_z = []
            for k, (wab, duw, dub) in enumerate(((wab1_b, du1T, du1_b), (wab2_b, du2T, du2_b))):
                a = pool.do(call(nc.gpsimd.memset, duT[k][:, :], 0.0))
                c = pool.do(call(nc.gpsimd.memset, dlT[k][:, :], 0.0))
                c = pool.do(call(nc.gpsimd.memset, dlT[k][32:33, :], 1.0), c)
                d = pool.do(call(nc.gpsimd.memset, gates_b[k][:, 0:DR], 0.0), c)
                f.dma(sp, duT[k][0:DR, :], duw, a)
                f.dma(sp, duT[k][32:33, :], dub.unsqueeze(0))
                t_c = f.dma(sp, gates_b[k][:, DR:ABW], wab.unsqueeze(0).broadcast_to([P, GATES]))
                t_z += [c, d]
            n32 = DCH * RD2
            z0 = pool.do(call(nc.gpsimd.memset, read2[:, DCH, :, :], 0.0))
            t_read2 = dve.do(call(nc.vector.tensor_tensor,
                read2[:, 0:DCH, :, :].rearrange("p a b c -> p (a b) c"),
                wrep[:, :].unsqueeze(2).broadcast_to([P, n32, HPC]),
                spread[:, :].unsqueeze(1).broadcast_to([P, n32, HPC]), ALU.mult), t_rep)

            yield

            mlp_banks = Banks([0, 1, 2, 3])
            one = Banks([6, 7])
            pair_read = [None]
            V, S, G = nc.vector, nc.scalar, nc.gpsimd

            used = {}

            def write(k, w, out_t, ab_t, out_ready, ab_ready, load_hs, scale_hs, tail):
                bank, free = one.take()
                t = pe.do(call(nc.tensor.transpose, ps[0:DR, bank, 0:P], ab_t[:, 0:DR], ident[:, :]), ab_ready, free)
                dl = dve.do(call(V.tensor_copy, dlT[k][0:DR, :], ps[0:DR, bank, 0:P]), t, used.get(("dlT", k)), *t_z)
                one.read[bank] = dl
                loads = load_hs()
                yield 0.2, 0, 0.4
                bank, free = one.take()
                t = pe.do(call(nc.tensor.matmul, ps[:, bank, :], dlT[k][:, :], duT[w][:, :], start=True, stop=True),
                          dl, free, t_c)
                used[("dlT", k)] = t
                d_v = dve.do(call(V.tensor_copy, delta[k][:, :], ps[:, bank, :]), t, used.get(("delta", k)))
                one.read[bank] = d_v
                a = act.do(call(S.activation, tmp[k][:, :], delta[k][:, :], ACT.Abs), d_v, used.get(("tmp", k)))
                a = act.do(call(S.activation, tmp[k][:, :], tmp[k][:, :], ACT.Exp, scale=-1.0), a)
                a_ln = act.do(call(S.activation, tmp[k][:, :], tmp[k][:, :], ACT.Ln, bias=1.0), a)
                al = ab_t[:, DR:DR + NA]
                g = g1[k]
                a = act.do(call(S.activation, g[:, 0, :], al, ACT.Abs), ab_ready, used.get(("gate", k)))
                a = act.do(call(S.activation, g[:, 0, :], g[:, 0, :], ACT.Exp, scale=-1.0), a)
                a = act.do(call(S.activation, g[:, 0, :], g[:, 0, :], ACT.Ln, bias=1.0), a)
                yield 0.9, 0, 2.8
                d_delta = dve.do(call(V.scalar_tensor_tensor,
                    out=delta[k][:, :], in0=delta[k][:, :], scalar=0.0, in1=tmp[k][:, :],
                    op0=ALU.max, op1=ALU.add), a_ln)
                d_sp = dve.do(call(V.scalar_tensor_tensor, out=g[:, 1, :], in0=al, scalar=0.0, in1=g[:, 0, :],
                                   op0=ALU.max, op1=ALU.add), a, used.get(("gate_sp", k)))
                A3 = Ab[k][:, :].rearrange("p (s r c) -> p s r c", s=HS, r=RH)
                A2 = Ab[k][:, :].rearrange("p (s n) -> p s n", s=HS)
                Ah = Ab[k][:, :].rearrange("p (h c) -> p h c", c=C - 1)
                dl3 = delta[k][:, :].rearrange("p (s r) -> p s r", s=HS).unsqueeze(3).broadcast_to([P, HS, RH, C - 1])
                sp3 = g[:, 1, :].rearrange("p (r c) -> p r c", r=RH).unsqueeze(1).broadcast_to([P, HS, RH, C - 1])
                gp = pool.do(call(G.tensor_tensor, A3, dl3, sp3, ALU.mult), d_delta, d_sp, used.get(("A", k)))
                used[("gate_sp", k)] = used[("delta", k)] = gp
                d = dve.do(call(V.tensor_scalar, g[:, 2, :], g[:, 1, :], -1.0, -SSM_EPS, ALU.mult, ALU.add), d_sp)
                d = dve.do(call(V.reciprocal, g[:, 3, :], g[:, 2, :]), d)
                d_gain = dve.do(call(V.tensor_tensor, g[:, 2, :], g[:, 3, :], ab_t[:, DR + NA:DR + 2 * NA],
                                     ALU.mult), d)
                yield 0, 2.8, 1.2
                a_A = act.do(call(S.activation, Ab[k][:, :], Ab[k][:, :], ACT.Exp, scale=-1.0), gp)
                hs_ready = scale_hs(loads)
                bs = ab_t[:, DR + 2 * NA:ABW].unsqueeze(1).broadcast_to([P, HS, RH])
                h4 = hs[k][:, :].rearrange("p (h c) -> p h c", c=C)
                d = dve.do(call(V.tensor_tensor, tmp[k][:, :].rearrange("p (s r) -> p s r", s=HS),
                                delta[k][:, :].rearrange("p (s r) -> p s r", s=HS), bs, ALU.mult), d_delta)
                d = dve.do(call(V.tensor_tensor, tmp[k][:, :], tmp[k][:, :], out_t[:, :], ALU.mult), d, out_ready)
                d_skip = dve.do(call(V.tensor_tensor, h4[:, :, C - 1], h4[:, :, C - 1], tmp[k][:, :], ALU.add),
                                d, hs_ready)
                used[("tmp", k)] = d_skip
                yield 0, 0, 1.6
                g_hs = pool.do(call(G.tensor_tensor, h4[:, :, 0:C - 1], h4[:, :, 0:C - 1], Ah, ALU.mult),
                               a_A, hs_ready)
                yield 0, 3.4, 0.1
                d = dve.do(call(V.scalar_tensor_tensor,
                    out=A2, in0=A2, scalar=1.0, in1=g[:, 2, :].unsqueeze(1).broadcast_to([P, HS, NA]),
                    op0=ALU.subtract, op1=ALU.mult), g_hs, d_gain)
                used[("gate", k)] = d
                d = dve.do(call(V.tensor_tensor, Ah, Ah, out_t[:, :].unsqueeze(2).broadcast_to([P, H, C - 1]),
                                ALU.mult), d)
                d_hs = dve.do(call(V.tensor_tensor, h4[:, :, 0:C - 1], h4[:, :, 0:C - 1], Ah, ALU.add),
                              d, g_hs, d_skip)
                used[("A", k)] = d_hs
                yield 0, 0, 5.2
                yield from tail(d_hs)

            hs_free = [[], []]
            hs_stored, y_ready, y_read, x2_stored = {}, {}, {}, {}

            class AttentionWrite:

                def __init__(self, k, tiles, oT, out, ab, hsT, banks):
                    self.k, self.oT, self.out, self.ab, self.hsT, self.banks = k, oT, out, ab, hsT, banks
                    self.hsT_read, self.banks_read, self.out_read = {}, (), ()
                    self.tiles = list(tiles)
                    self.load(None)

                def load(self, free):
                    self.oT_loaded = flow(f"m_oT{self.k}").dma(sp, self.oT, oT_d[self.tiles.pop(0)], free)

            def attention_write(i, z):
                k, (b0, b1) = z.k, z.banks
                H_ = hs[k]
                lo_ = z.oT_loaded

                def load_hs():
                    return flow(f"m_hs{k}").dma(sp, H_[:, :], x[i], *hs_free[k])

                def scale_hs(loaded):
                    return act.do(call(S.activation, H_[:, :], H_[:, :], ACT.Identity,
                                       bias=nmr1[:, i:i + 1], scale=rstd1[:, i:i + 1]), loaded)

                for c0, cn, bank in ((0, H, b0), (H, ABW, b1)):
                    for kc in range(HCH):
                        mk = call(nc.tensor.matmul,
                            ps[:, bank, 0:cn], z.oT[:, kc, :], wod1[:, kc, c0:c0 + cn],
                            start=(kc == 0), stop=(kc == HCH - 1))
                        if bank == b1 and kc == HCH - 1:
                            t = pe.do(mk)
                        else:
                            pe.quiet(mk, lo_, t_wod1, *z.banks_read)
                if z.tiles:
                    z.load(t)
                a_out = act.do(call(S.activation, z.out[:, :], ps[:, b0, :], ACT.Copy), t, *z.out_read)
                d_ab = dve.do(call(V.tensor_tensor, z.ab[:, :], ps[:, b1, 0:ABW], gates_b[0][:, :], ALU.add),
                              t, t_c, *t_z, *z.out_read)
                z.banks_read = (a_out, d_ab)
                yield 4.4, 0, 0.6

                def tail(d_hs):
                    z.out_read = (d_hs,)
                    hs_stored[i] = flow(f"m_hs_store{k}").dma(sp, hs_d[i], H_[:, :], d_hs)
                    q2 = RD2 * HPC
                    turned = []
                    for q in range(4):
                        bank, free = one.take()
                        for j in range(4):
                            mk = call(nc.tensor.transpose,
                                ps[:, bank, P * j:P * j + P], H_[:, P * (4 * q + j):P * (4 * q + j) + P], ident[:, :])
                            if j < 3:
                                pe.quiet(mk, d_hs, free)
                            else:
                                t = pe.do(mk)
                        if q % 2:
                            r = act.do(call(S.activation, z.hsT[q], ps[:, bank, :], ACT.Copy), t, z.hsT_read.get(q))
                        else:
                            r = dve.do(call(V.tensor_copy, z.hsT[q], ps[:, bank, :]), t, z.hsT_read.get(q))
                        one.read[bank] = r
                        turned.append(r)
                        if q % 2:
                            yield 1.0, 0, 0.2
                    hs_free[k][:] = [t, hs_stored[i]]
                    for q in range(4):
                        for j in range(4):
                            jj = 4 * q + j
                            n = q2 if jj % 8 == 7 else q2 + 32
                            mk = call(nc.tensor.matmul,
                                ps[:, b0 + jj // 8, q2 * (jj % 8):q2 * (jj % 8) + n], z.hsT[q][:, P * j:P * j + P],
                                read2[:, jj:jj + 2, :, :].rearrange("p a b c -> p (a b c)")[:, 0:n],
                                start=True, stop=True)
                            if j < 3:
                                pe.quiet(mk, turned[q], t_read2, z0, *z.banks_read)
                            else:
                                t = pe.do(mk)
                        z.hsT_read[q] = t
                    yield 3.8, 0, 0.2
                    yv = ps[:, b0:b0 + 2, :].rearrange("p a (j o h) -> p a j o h", o=RD2, h=HPC)
                    for o in range(RD2):
                        for a_ in range(2):
                            d = dve.do(call(V.bn_stats, st[:, k, o, a_, :], yv[:, a_, :, o, :]), t)
                    for o in range(RD2):
                        d2 = dve.do(call(V.bn_aggr, my[:, k, o, :], st[:, k, o, :, :]), d)
                    d = dve.do(call(V.tensor_scalar, sc[:, k, 0, :], my[:, k, :, 1], EPS, None, ALU.add), d2,
                               used.get(("sc", k)))
                    g = power_mhalf(sc[:, k, 1, :], sc[:, k, 0, :], d)
                    yield 0, 0, 2.2
                    d = dve.do(call(V.scalar_tensor_tensor,
                        out=sc[:, k, 2, :], in0=my[:, k, :, 0], scalar=-1.0, in1=sc[:, k, 1, :],
                        op0=ALU.mult, op1=ALU.mult), g)
                    y = y2[i % TB]
                    for o in range(RD2):
                        for a_ in range(2):
                            a = act.do(call(S.activation,
                                y[:, o, 256 * a_:256 * a_ + 256].rearrange("p (j h) -> p j h", h=HPC),
                                yv[:, a_, :, o, :], ACT.Identity, bias=sc[:, k, 2, o:o + 1],
                                scale=sc[:, k, 1, o:o + 1]), d, y_read.get(i - TB))
                    used[("sc", k)] = a
                    z.banks_read = (a,)
                    y_ready[i] = a
                    yield 0, 0, 1.5
                yield from write(k, 0, z.out, z.ab, a_out, d_ab, load_hs, scale_hs, tail)

            slot_read, mlp_out = {}, {}

            def mlp_write(i, k):
                def load_hs():
                    return (flow(f"m_hs{k}").dma(sp, hs[k][:, :], hs_d[i], hs_stored[i], *hs_free[k]),
                            flow(f"m_x{k}").dma(sp, xt[k][:, :], x[i], used.get(("x", k))))

                def tail(d_hs):
                    slot_read[i] = d_hs
                    g = pool.do(call(G.tensor_tensor, hs[k][:, :], hs[k][:, :], xt[k][:, :], ALU.add), d_hs)
                    used[("x", k)] = g
                    yield 0, 4.5, 0.1
                    x2_stored[i] = flow(f"m_x2_store{k}").dma(sp, x2_d[i], hs[k][:, :], g)
                    hs_free[k][:] = [x2_stored[i]]
                def join(loaded):
                    pool.wait(loaded[1])
                    return loaded[0]

                a_out, d_ab = mlp_out[i]
                yield from write(k, 1, outs2[i % TB], ab2[i % TB], a_out, d_ab, load_hs, join, tail)

            yT_ready, yT_free, yraw_read = {}, [None], {}

            def turn(blk):
                for k in range(RD2 * HCH):
                    o, hc = divmod(k, HCH)
                    bank, free = one.take()
                    for q in range(TB):
                        i = blk * TB + q
                        mk = call(nc.tensor.transpose,
                            ps[:, bank, P * q:P * q + P], y2[q][:, o, P * hc:P * hc + P], ident[:, :])
                        if q < TB - 1:
                            pe.quiet(mk, y_ready[i], free)
                        else:
                            t = pe.do(mk, y_ready[i])
                    s = k % 2
                    d = dve.do(call(V.tensor_scalar,
                        yraw[s][:, :], ps[:, bank, :], gam[:, k:k + 1], bet[:, k:k + 1], ALU.mult, ALU.add),
                        t, yraw_read.get(s), t_read2, t_c)
                    one.read[bank] = d
                    a = act.do(call(S.activation, yhi[:, k, :], yraw[s][:, :], ACT.Copy), d, yT_free[0])
                    g = pool.do(call(G.tensor_tensor,
                        ylo[:, k, :], yraw[s][:, :], yhi[:, k, :].bitcast(F32), ALU.subtract), a)
                    yraw_read[s] = g
                    yT_ready[(blk, k)] = g
                for q in range(TB):
                    y_read[blk * TB + q] = t

            win_read, win_loaded, win_turn = {}, {}, [0]
            w2_read, w2_loaded, w2_turn = {}, {}, [0]
            units = [(g2, mc) for _ in range(NBLK) for m2 in range(0, MCH, 2) for g2 in range(2)
                     for mc in (m2, m2 + 1)]

            def load_win(n):
                if n < len(units):
                    g2, mc = units[n]
                    s = n % WR
                    win_loaded[n] = flow(f"m_win{s}").dma(
                        sp, win[s][:, :, :, :].rearrange("p a c m -> p a (c m)"), win_d[2 * mc + g2],
                        win_read.get(n - WR))

            def load_w2(n):
                if n < NBLK * (TB // 2) * MCH:
                    s = n % W2R
                    w2_loaded[n] = flow(f"m_w2_{s}").dma(sp, w2[s][:, :], wod2T[n % MCH], w2_read.get(n - W2R))

            silu_read, hT_free, after = {}, [None], []

            def mlp(blk):
                hready = {}
                for m2 in range(0, MCH, 2):
                    got = {}
                    for g2 in range(2):
                        for mc in (m2, m2 + 1):
                            n = win_turn[0]
                            win_turn[0] += 1
                            s = n % WR
                            bank, free = mlp_banks.take()
                            for ic in range(HCH):
                                k = g2 * HCH + ic
                                for p3, (wl, y) in enumerate(((0, yhi), (0, ylo), (1, yhi))):
                                    mk = call(nc.tensor.matmul,
                                        ps[:, bank, :], win[s][:, wl, ic, :], y[:, k, :],
                                        start=(ic == 0 and p3 == 0), stop=(ic == HCH - 1 and p3 == 2))
                                    ws = (win_loaded[n], yT_ready[(blk, k)], free)
                                    if ic == HCH - 1 and p3 == 2:
                                        t = pe.do(mk, *ws)
                                    else:
                                        pe.quiet(mk, *ws)
                            win_read[n] = t
                            load_win(n + WR)
                            got[(g2, mc)] = (bank, t)
                            if g2 == 1:
                                s2 = mc % 2
                                d = dve.do(call(V.tensor_tensor,
                                    hT[:, mc, :], silu[s2][:, :], ps[:, bank, :], ALU.mult), t, a2[mc], hT_free[0])
                                silu_read[s2] = d
                                mlp_banks.read[bank] = d
                                hready[mc] = d
                            elif mc % 2:
                                a2 = {}
                                for m in (m2, m2 + 1):
                                    gb, tg = got[(0, m)]
                                    s2 = m % 2
                                    a2[m] = act.do(call(S.activation,
                                        silu[s2][:, :], ps[:, gb, :], ACT.Silu), tg, silu_read.get(s2))
                                    mlp_banks.read[gb] = a2[m]
                                act.queue.append(call(S.preload_act_table_set, "natural_log_exp_and_others"))
                            yield 2.8
                yT_free[0] = t
                if blk == NBLK - 1:
                    place[0] = experts_place
                    after.append(experts(one, x2_stored, t, first_loads_end, xt))
                for q2 in range(TB // 2):
                    frees = [mlp_banks.read[k] for k in range(4)]
                    for k in range(MCH):
                        n = w2_turn[0]
                        w2_turn[0] += 1
                        s = n % W2R
                        for e in range(2):
                            q = 2 * q2 + e
                            for c0, cn, bank in ((0, H, 2 * e), (H, ABW, 2 * e + 1)):
                                mk = call(nc.tensor.matmul,
                                    ps[:, bank, 0:cn], hT[:, k, P * q:P * q + P], w2[s][:, c0:c0 + cn],
                                    start=(k == 0), stop=(k == MCH - 1))
                                ws = (hready[k], w2_loaded[n], *frees)
                                if bank == 3 or k == MCH - 1 and bank == 1:
                                    t = pe.do(mk, *ws)
                                else:
                                    pe.quiet(mk, *ws)
                            if k == MCH - 1:
                                i, r = blk * TB + q, slot_read.get((blk - 1) * TB + q)
                                assert blk == 0 or r is not None
                                a_out = act.do(call(S.activation,
                                    outs2[q][:, :], ps[:, 2 * e, :], ACT.Copy), t, r)
                                d_ab = dve.do(call(V.tensor_tensor,
                                    ab2[q][:, :], ps[:, 2 * e + 1, 0:ABW], gates_b[1][:, :], ALU.add), t, r)
                                mlp_banks.read[2 * e], mlp_banks.read[2 * e + 1] = a_out, d_ab
                                mlp_out[i] = (a_out, d_ab)
                        w2_read[n] = t
                        load_w2(n + W2R)
                        if after and k % 4 == 1 and q2 * MCH + k < 4 * 5:
                            next(after[0])
                        yield 2.25
                hT_free[0] = t

            def attention_writes(tiles, z):
                for i in tiles:
                    yield from attention_write(i, z)

            def mlp_writes(tiles, k):
                for i in tiles:
                    yield from mlp_write(i, k)

            lanes = [AttentionWrite(0, [*range(0, TB, 2), *range(TB, NT)], oTt[:, :, :], outs1, ab1,
                                    [tT[:, q, :] for q in range(4)], (4, 5))]
            for n in range(WR):
                load_win(n)
            for n in range(W2R):
                load_w2(n)
            yield
            lanes.append(AttentionWrite(1, range(1, TB, 2), hT[:, 0, :].rearrange("p (a b) -> p a b", b=P),
                                        outs2[0], ab2[0], [hT[:, 1 + q, :] for q in range(4)], (2, 3)))
            weave(None, attention_writes(range(0, TB, 2), lanes[0]), attention_writes(range(1, TB, 2), lanes[1]))
            hT_free[0] = lanes[1].hsT_read[3]
            for bank in lanes[1].banks:
                mlp_banks.read[bank] = lanes[1].banks_read[0]
            turn(0)
            for blk in range(NBLK):
                sides = []
                if blk:
                    sides.append(mlp_writes(range((blk - 1) * TB, blk * TB), 1))
                if blk + 1 < NBLK:
                    sides.append(attention_writes(range((blk + 1) * TB, (blk + 2) * TB), lanes[0]))
                weave(mlp(blk), *sides)
                if blk + 1 < NBLK:
                    turn(blk + 1)
            barrier()
            one.banks.append(5)
            one.read[5] = None
            last = range((NBLK - 1) * TB, NT)
            next(after[0])
            weave(after[0], mlp_writes(last[0::2], 1), mlp_writes(last[1::2], 0))

        def experts(outb, x2_stored, free, end, other_x):
            SCALE = 2.0 * NE
            wA = sb("e_A", [P, DCH, EW + NE])
            wB = sb("e_B", [P, D])
            brb = sb("e_br", [P, NE])
            XR = 9
            xt = [sb(f"e_x{k}", [P, D]) for k in range(3)]
            assert place[0] <= end
            x_free, loaded = {}, {}

            def load(i, free=None):
                if i < NT:
                    loaded[i] = flow(f"e_x{i % XR}").dma(
                        sp, xt[i % XR][:, :], x2_d[i], x_free.get(i - XR), x2_stored[i], free)

            for n in range(3):
                load(n, free)
                yield
            t_A = flow("e_A").dma(sp, wA[:, :, :], expA)
            yield
            flow("e_B").dma(sp, wB[:, :], expB)
            t_B = flow("e_B").dma(sp, brb[:, :], br.unsqueeze(0).broadcast_to([P, NE]))
            yield
            other_x[0] = sb("m_x_other", [P, D])
            xt += [sb(f"e_x{k}", [P, D]) for k in range(3, XR)]
            xT_ = [sb(f"e_xT{k}", [P, DCH, P]) for k in range(2)]
            ones = sb("e_ones", [P, P])
            asum = sb("e_Asum", [P, EW + NE])
            st = [sb(f"e_stats{k}", [P, 4, 6]) for k in range(2)]
            mv = [sb(f"e_moments{k}", [P, 8]) for k in range(4)]
            low = [sb(f"e_low{k}", [P, EW + NE]) for k in range(2)]
            lw = [sb(f"e_weighted{k}", [P, EW]) for k in range(2)]
            rt = [sb(f"e_router{k}", [P, 3, NE]) for k in range(2)]
            lT = [sb(f"e_lowT{k}", [P, P]) for k in range(2)]
            assert place[0] <= plan_end["mix_weights"]
            V, S, G = nc.vector, nc.scalar, nc.gpsimd
            c1 = pool.do(call(G.memset, ones[:, :], 1.0))
            yield 0
            turned, lowb = Banks([0, 1, 2]), Banks([3, 4])
            norm, xT_ready, xT_read = {}, {}, {}
            low_read, lw_ready, lw_read, lT_ready, lT_read = {}, {}, {}, {}, {}

            def stage_stats(i):
                if i >= NT:
                    return
                s = i % 2
                X = xt[i % XR]
                for q in range(4):
                    d = dve.do(call(V.bn_stats, st[s][:, q, :], X[:, 512 * q:512 * q + 512]), loaded[i])
                m = mv[i % 4]
                d = dve.do(call(V.bn_aggr, m[:, 0:2], st[s][:, :, :]), d)
                d1 = dve.do(call(V.tensor_scalar, m[:, 2:3], m[:, 0:1], -1.0, None, ALU.mult), d)
                d = dve.do(call(V.tensor_scalar, m[:, 3:4], m[:, 1:2], EPS, None, ALU.add), d)
                norm[i] = (d1, power_mhalf(m[:, 4:5], m[:, 3:4], d))

            def stage_transpose(i):
                s = i % 2
                X = xt[i % XR]
                ready = []
                for q in range(4):
                    bank, free = turned.take()
                    for j in range(4):
                        mk = call(nc.tensor.transpose,
                            ps[:, bank, P * j:P * j + P], X[:, P * (4 * q + j):P * (4 * q + j) + P], ident[:, :])
                        t = (pe.do if j == 3 else pe.quiet)(mk, loaded[i], free)
                    dst = xT_[s][:, 4 * q:4 * q + 4, :].rearrange("p a b -> p (a b)")
                    r = act.do(call(S.activation, dst, ps[:, bank, :], ACT.Copy), t, xT_read.get(i - 2))
                    turned.read[bank] = r
                    ready.append(r)
                xT_ready[i] = ready

            def stage_low(i):
                s = i % 2
                m = mv[i % 4]
                bank, free = lowb.take()
                for j in range(DCH):
                    mk = call(nc.tensor.matmul, ps[:, bank, 0:EW + NE], xT_[s][:, j, :], wA[:, j, :],
                                                      start=(j == 0), stop=(j == DCH - 1))
                    t = (pe.do if j == DCH - 1 else pe.quiet)(mk, xT_ready[i][j // 4], free)
                xT_read[i] = t
                n1, n2 = norm[i]
                d = dve.do(call(V.scalar_tensor_tensor,
                    out=low[s][:, :], in0=asum[:, :], scalar=m[:, 2:3], in1=ps[:, bank, 0:EW + NE],
                    op0=ALU.mult, op1=ALU.add), t, n1, t_asum)
                lowb.read[bank] = d
                r = rt[s]
                d = dve.do(call(V.scalar_tensor_tensor,
                    out=r[:, 0, :], in0=low[s][:, EW:EW + NE], scalar=m[:, 4:5], in1=brb[:, :],
                    op0=ALU.mult, op1=ALU.add), d, n2, t_B)
                d = dve.do(call(V.tensor_reduce, m[:, 5:6], r[:, 0, :], AX_X, ALU.max, negate=True), d)
                a = act.do(call(S.activation, r[:, 1, :], r[:, 0, :], ACT.Exp, bias=m[:, 5:6],
                                                accum_out=m[:, 6:7]), d)
                d = dve.do(call(V.reciprocal, m[:, 7:8], m[:, 6:7]), a)
                d = dve.do(call(V.tensor_scalar, r[:, 2, :], r[:, 1, :], m[:, 7:8], SCALE, ALU.mult, ALU.mult), d)
                lw_ready[i] = dve.do(call(V.scalar_tensor_tensor,
                    out=lw[s][:, :].rearrange("p (e r) -> p e r", e=NE),
                    in0=low[s][:, 0:EW].rearrange("p (e r) -> p e r", e=NE), scalar=m[:, 4:5],
                    in1=r[:, 2, :].unsqueeze(2).broadcast_to([P, NE, RANK]), op0=ALU.mult, op1=ALU.mult),
                    d, lw_read.get(i - 2))

            def stage_turn(i):
                s = i % 2
                bank, free = lowb.take()
                t = pe.do(call(nc.tensor.transpose, ps[:, bank, 0:P], lw[s][:, :], ident[:, :]), lw_ready[i], free)
                lw_read[i] = t
                lT_ready[i] = act.do(call(S.activation, lT[s][:, :], ps[:, bank, 0:P], ACT.Copy),
                                     t, lT_read.get(i - 2))
                lowb.read[bank] = lT_ready[i]

            def stage_out(i):
                s = i % 2
                X = xt[i % XR]
                for q in range(4):
                    bank, free = outb.take()
                    t = pe.do(call(nc.tensor.matmul,
                        ps[:, bank, :], lT[s][:, :], wB[:, 512 * q:512 * q + 512], start=True, stop=True),
                        lT_ready[i], free, t_B)
                    d = dve.do(call(V.tensor_tensor,
                        X[:, 512 * q:512 * q + 512], ps[:, bank, :], X[:, 512 * q:512 * q + 512], ALU.add), t)
                    outb.read[bank] = d
                lT_read[i] = t
                x_free[i] = flow(f"e_out{i % XR}").dma(sp, out[i], X[:, :], d)

            for n in range(3, XR - 3):
                load(n)
            stage_transpose(0)
            stage_stats(0)
            stage_stats(1)
            yield 1.9
            bank, _ = lowb.take()
            for j in range(DCH):
                t = pe.do(call(nc.tensor.matmul, ps[:, bank, 0:EW + NE], ones[:, :], wA[:, j, :],
                               start=(j == 0), stop=(j == DCH - 1)), t_A, c1)
            t_asum = dve.do(call(V.tensor_copy, asum[:, :], ps[:, bank, 0:EW + NE]), t)
            lowb.read[bank] = t_asum
            yield 4.0
            for n in range(NT + 3):
                if 0 < n < NT:
                    stage_transpose(n)
                    stage_stats(n + 1)
                    yield 1.9
                if 0 <= n - 2 < NT:
                    stage_turn(n - 2)
                if 0 <= n - 1 < NT:
                    stage_low(n - 1)
                    yield 4.0
                if 0 <= n - 3 < NT:
                    stage_out(n - 3)
                    yield 3.5
                load(n + XR - 3)

        project()
        sp.wait(*[f.last() for f in flows.values()])

        block = ctx.enter_context(nc.Block())

        def run(lane):
            for make in lane.queue:
                make()

        @block.tensor
        def _(e):
            run(pe)

        @block.scalar
        def _(e):
            run(act)

        @block.vector
        def _(e):
            run(dve)

        @block.gpsimd
        def _(e):
            run(pool)

        @block.sync
        def _(e):
            run(sp)


def kernel(x, pos_BxS, ctx_1024, L0_xattn_attn_read_w, L0_xattn_attn_read_g, L0_xattn_attn_read_b,
           L0_xattn_qkv_w, L0_xattn_attn_wod_w, L0_xattn_attn_wab_w, L0_xattn_attn_wab_b,
           L0_xattn_attn_du_w, L0_xattn_attn_du_b, L0_xattn_mlp_read_w, L0_xattn_mlp_read_g,
           L0_xattn_mlp_read_b, L0_xattn_mlp_wod_w, L0_xattn_mlp_wab_w, L0_xattn_mlp_wab_b,
           L0_xattn_mlp_du_w, L0_xattn_mlp_du_b, L0_ffn_A, L0_ffn_B, L0_ffn_Wr, L0_ffn_br):
    import concourse.bacc as bacc
    from concourse.bass_utils import run_bass_kernel_spmd

    def lay(a):
        return np.ascontiguousarray(a)

    def cols(w, n):
        return lay(np.transpose(np.reshape(w, (w.shape[0], n, P)), (2, 1, 0)))

    order = np.arange(H).reshape(NH, 2, HALF).transpose(1, 0, 2).reshape(-1)
    wqkv = np.asarray(L0_xattn_qkv_w)
    qkv = np.concatenate([cols(wqkv[0][order], HCH), cols(wqkv[1][order], HCH), cols(wqkv[2], HCH)], axis=1)

    def read_rep(w, outs):
        return lay(np.transpose(np.reshape(w, (DCH, HPC, outs, C)), (1, 3, 0, 2)).reshape(P, DCH * outs))

    xs = np.reshape(x, (NT, P, D))
    ctx = np.reshape(ctx_1024, (2, MCH, P, HCH, P))
    freq = (1.0 / 10000.0 ** (np.arange(HALF, dtype=np.float64) / HALF)).astype(np.float32)
    arrays = {
        "x": lay(xs),
        "xT": lay(np.transpose(np.reshape(x, (NT, P, DCH, P)), (0, 3, 2, 1))),
        "pos": lay(np.reshape(pos_BxS, (T,))),
        "inv_freq": lay(np.tile(freq, P // HALF).reshape(P, 1)),
        "ident": np.eye(P, dtype=np.float32),
        "causal": lay(np.where(np.arange(P)[None, :] > np.arange(P)[:, None], np.float32(NEG), np.float32(0))),
        "spread": lay((np.arange(P)[:, None] // C == np.arange(HPC)[None, :]).astype(np.float32)),
        "read1": read_rep(L0_xattn_attn_read_w, RD1),
        "gamma1": lay(np.reshape(L0_xattn_attn_read_g, (RD1 * HCH, P)).T),
        "beta1": lay(np.reshape(L0_xattn_attn_read_b, (RD1 * HCH, P)).T),
        "qkvT": lay(qkv),
        "wod1T": cols(np.concatenate([L0_xattn_attn_wod_w, L0_xattn_attn_wab_w], axis=0), HCH),
        "wab1_b": lay(L0_xattn_attn_wab_b),
        "du1T": lay(np.transpose(L0_xattn_attn_du_w)),
        "du1_b": lay(L0_xattn_attn_du_b),
        "read2": read_rep(L0_xattn_mlp_read_w, RD2),
        "gamma2": lay(np.reshape(L0_xattn_mlp_read_g, (RD2 * HCH, P)).T),
        "beta2": lay(np.reshape(L0_xattn_mlp_read_b, (RD2 * HCH, P)).T),
        "mlp_inT": lay(np.transpose(ctx, (1, 0, 4, 3, 2)).reshape(2 * MCH, P, HCH * P)),
        "wod2T": lay(np.transpose(np.concatenate([L0_xattn_mlp_wod_w, L0_xattn_mlp_wab_w], axis=0)).reshape(
            MCH, P, WOD)),
        "wab2_b": lay(L0_xattn_mlp_wab_b),
        "du2T": lay(np.transpose(L0_xattn_mlp_du_w)),
        "du2_b": lay(L0_xattn_mlp_du_b),
        "expA": cols(np.concatenate([np.reshape(L0_ffn_A, (EW, D)), L0_ffn_Wr], axis=0), DCH),
        "expB": lay(np.transpose(L0_ffn_B, (0, 2, 1)).reshape(EW, D)),
        "br": lay(L0_ffn_br),
    }
    nc = bacc.Bacc("TRN2", target_bir_lowering=False, num_devices=1)
    named, args = {}, []
    for name, a in arrays.items():
        named[f"in_{name}"] = a
        args.append(nc.dram_tensor(f"in_{name}", a.shape, mybir.dt.from_np(a.dtype), kind="ExternalInput").ap())
    out = nc.dram_tensor("out_x", [NT, P, D], F32, kind="ExternalOutput").ap()
    program(nc, *args, out)
    got = run_bass_kernel_spmd(nc, [named], core_ids=[0])
    return got.results[0]["out_x"].reshape(B, L, D)
```
